# Optimizing a Trainium2 kernel written in Bass

```python
import numpy as np
import jax
import jax.numpy as jnp

def _softmax(x, axis=-1):
    return jax.nn.softmax(x, axis=axis)

def _gelu(x):
    return jax.nn.gelu(x, approximate=True)

def _silu(x):
    return jax.nn.silu(x)

def _sigmoid(x):
    return jax.nn.sigmoid(x)

def _layernorm(x, axis=-1, eps=1e-05):
    m = jnp.mean(x, axis=axis, keepdims=True)
    v = jnp.var(x, axis=axis, keepdims=True)
    return (x - m) / jnp.sqrt(v + eps)

def _scatter_add(tgt, idx, src, axis=0):
    return tgt.at[idx].add(src)

def _segment_sum(src, seg, n):
    return jax.ops.segment_sum(src, seg, n)
kernel_name = 'mk_flamingo_gated_d1_seqx_r2_c6c78f'

def setup_inputs(seed: int=0):
    np.random.seed(seed)
    _w = jnp.asarray

    def _rec_inputs():
        import jax
        import jax.numpy as jnp
        _rk = jax.random.key(seed)
        x = -0.0002928 + 1 * jax.random.normal(jax.random.fold_in(_rk, 1), (8, 512, 512), jnp.float32)
        _lenS = 512 - jax.random.randint(jax.random.fold_in(_rk, 7), (8,), 0, max(1, 512 // 4) + 1, jnp.int32)
        _lenS2 = 512 - jax.random.randint(jax.random.fold_in(_rk, 8), (8,), 0, max(1, 512 // 4) + 1, jnp.int32)
        _ctx_1024P = jax.random.normal(jax.random.fold_in(_rk, 11), (8, 16, 512), jnp.float32)
        _ctx_1024c = jax.random.dirichlet(jax.random.fold_in(_rk, 511), 0.3 * jnp.ones((16,), jnp.float32), (8, 512))
        _ctx_1024t = jnp.einsum('bsk,bkd->bsd', _ctx_1024c, _ctx_1024P)
        _ctx_1024t = _ctx_1024t * jax.lax.rsqrt(jnp.mean(jnp.square(_ctx_1024t)) + 1e-12) * 0.953939
        ctx_1024 = -1.52775e-05 + 0.999936 * (_ctx_1024t + 0.3 * jax.random.normal(jax.random.fold_in(_rk, 611), (8, 512, 512), jnp.float32))
        _g = jax.random.normal(jax.random.fold_in(_rk, 9001), (2, 1), jnp.float32)
        _g = jnp.sign(_g) * jnp.maximum(jnp.abs(_g), 1.0) + (_g == 0) * 1.0
        g_xattn = _g[0]
        g_ffn = _g[1]
        return (x, ctx_1024, g_xattn, g_ffn)
    x, ctx_1024, g_xattn, g_ffn = _rec_inputs()

    def _L0_xattn_setup():
        import jax, jax.numpy as jnp
        import numpy as np
        DIM = 512
        NUM_HEADS = 8
        HEAD_DIM = 64
        INNER = NUM_HEADS * HEAD_DIM
        key = jax.random.key(seed)
        ks = jax.random.split(key, 7)
        B, N, M = (8, 256, 2048)
        x = jax.random.normal(ks[0], (B, N, DIM), dtype=jnp.float32)
        context = jax.random.normal(ks[1], (B, M, DIM), dtype=jnp.float32)
        s_in = 1.0 / np.sqrt(DIM)
        s_inner = 1.0 / np.sqrt(INNER)
        Wq = jax.random.normal(ks[2], (DIM, INNER), dtype=jnp.float32) * s_in
        Wk = jax.random.normal(ks[3], (DIM, INNER), dtype=jnp.float32) * s_in
        Wv = jax.random.normal(ks[4], (DIM, INNER), dtype=jnp.float32) * s_in
        Wo = jax.random.normal(ks[5], (INNER, DIM), dtype=jnp.float32) * s_inner
        bo = jax.random.normal(ks[6], (DIM,), dtype=jnp.float32) * 0.01
        return {'x': x, 'context': context, 'Wq': Wq, 'Wk': Wk, 'Wv': Wv, 'Wo': Wo, 'bo': bo}
    _L0_xattn_all = _L0_xattn_setup()
    _L0_xattn_in = {k: v for k, v in _L0_xattn_all.items() if k in ('Wq', 'Wk', 'Wv', 'Wo', 'bo')}
    del _L0_xattn_all

    def _L0_ffn_setup():
        import jax, jax.numpy as jnp
        import numpy as np
        B, N, D, E, R, K = (4, 1024, 512, 8, 128, 2)
        key = jax.random.key(seed)
        ks = jax.random.split(key, 5)
        scale = 0.02
        return {'x': jax.random.normal(ks[0], (B, N, D), dtype=jnp.float32), 'gate_w': jax.random.normal(ks[1], (D, E), dtype=jnp.float32) * scale, 'Wu': jax.random.normal(ks[2], (E, D, R), dtype=jnp.float32) * scale, 'Wv': jax.random.normal(ks[3], (E, D, R), dtype=jnp.float32) * scale, 'Wo': jax.random.normal(ks[4], (E, R, D), dtype=jnp.float32) * scale}
    _L0_ffn_all = _L0_ffn_setup()
    _L0_ffn_in = {k: v for k, v in _L0_ffn_all.items() if k in ('gate_w', 'Wu', 'Wv', 'Wo')}
    del _L0_ffn_all
    return {'x': x, 'ctx_1024': ctx_1024, 'g_xattn': g_xattn, 'g_ffn': g_ffn, 'L0_xattn_Wq': _L0_xattn_in['Wq'], 'L0_xattn_Wk': _L0_xattn_in['Wk'], 'L0_xattn_Wv': _L0_xattn_in['Wv'], 'L0_xattn_Wo': _L0_xattn_in['Wo'], 'L0_xattn_bo': _L0_xattn_in['bo'], 'L0_ffn_gate_w': _L0_ffn_in['gate_w'], 'L0_ffn_Wu': _L0_ffn_in['Wu'], 'L0_ffn_Wv': _L0_ffn_in['Wv'], 'L0_ffn_Wo': _L0_ffn_in['Wo']}

def reference(x, ctx_1024, g_xattn, g_ffn, L0_xattn_Wq, L0_xattn_Wk, L0_xattn_Wv, L0_xattn_Wo, L0_xattn_bo, L0_ffn_gate_w, L0_ffn_Wu, L0_ffn_Wv, L0_ffn_Wo):
    import jax
    import jax.numpy as jnp

    def _L0_xattn_ref(x, context, Wq, Wk, Wv, Wo, bo):
        import jax, jax.numpy as jnp
        import numpy as np
        DIM = 512
        NUM_HEADS = 8
        HEAD_DIM = 64
        INNER = NUM_HEADS * HEAD_DIM
        B, N, _ = x.shape
        M = context.shape[1]
        scale = HEAD_DIM ** (-0.5)
        q = (x @ Wq).reshape(B, N, NUM_HEADS, HEAD_DIM).transpose(0, 2, 1, 3)
        k = (context @ Wk).reshape(B, M, NUM_HEADS, HEAD_DIM).transpose(0, 2, 1, 3)
        v = (context @ Wv).reshape(B, M, NUM_HEADS, HEAD_DIM).transpose(0, 2, 1, 3)
        attn = jax.nn.softmax(jnp.einsum('bhnd,bhmd->bhnm', q, k) * scale, axis=-1)
        out = jnp.einsum('bhnm,bhmd->bhnd', attn, v)
        out = out.transpose(0, 2, 1, 3).reshape(B, N, INNER)
        return out @ Wo + bo

    def _L0_ffn_ref(x, gate_w, Wu, Wv, Wo):
        import jax, jax.numpy as jnp
        import numpy as np
        B, N, D, E, R, K = (4, 1024, 512, 8, 128, 2)
        logits = jnp.einsum('bnd,de->bne', x, gate_w)
        topv, topi = jax.lax.top_k(logits, K)
        w = jax.nn.softmax(topv, axis=-1)
        u = jnp.einsum('bnd,edr->bner', x, Wu)
        v = jnp.einsum('bnd,edr->bner', x, Wv)
        s = jax.nn.silu(u) * v
        Y = jnp.einsum('bner,erd->bned', s, Wo)
        y_sel = jnp.take_along_axis(Y, topi[..., None], axis=2)
        out = jnp.einsum('bnkd,bnk->bnd', y_sel, w)
        return out
    x = x + jnp.tanh(g_xattn[0]) * _L0_xattn_ref(_layernorm(x, axis=-1), ctx_1024, L0_xattn_Wq, L0_xattn_Wk, L0_xattn_Wv, L0_xattn_Wo, L0_xattn_bo)
    x = x + jnp.tanh(g_ffn[0]) * _L0_ffn_ref(_layernorm(x, axis=-1), L0_ffn_gate_w, L0_ffn_Wu, L0_ffn_Wv, L0_ffn_Wo)
    return x

_drawn_inputs = setup_inputs


def setup_inputs(seed=0):
    import zlib

    import numpy as np

    out = dict(_drawn_inputs(seed))
    spreads = {}
    factors = {'L0_xattn_bo': 7.786,
     'L0_ffn_gate_w': 4.291,
     'L0_ffn_Wu': 3.765,
     'L0_ffn_Wv': 3.693,
     'L0_ffn_Wo': 3.691}
    for name, (base, spread) in spreads.items():
        noise = np.random.default_rng([zlib.crc32(name.encode()), seed]).standard_normal(out[name].shape)
        drawn = base * np.exp(spread * noise) if base else spread * noise
        out[name] = jnp.asarray(drawn.astype(out[name].dtype))
    for name, factor in factors.items():
        out[name] = (out[name] * factor).astype(out[name].dtype)
    return out
```

```python
import concourse.bass as bass
from concourse import mybir
from contextlib import ExitStack

F32 = mybir.dt.float32
F16 = mybir.dt.float16
I32 = mybir.dt.int32
U32 = mybir.dt.uint32
ALU = mybir.AluOpType
ACT = mybir.ActivationFunctionType
AXX = mybir.AxisListType.X

P = 128
XS = 16.0
WS = 256.0
EPS = 1e-5
RSQRT_SEED = float(0x5F3759DF)
NEWTON = 3
LN_CHAIN = 7 + 2 * NEWTON


class Count:

    def __init__(self, value=0):
        self.set(value, value)

    def set(self, value, parity):
        self.value, self.parity = value, parity

    def take(self, n=1):
        now, self.bank = self.value, self.parity % 2
        self.value, self.parity = now + n, self.parity + n
        return now


def since(eng, sem, count):
    if not isinstance(count, int) or count > 0:
        eng.wait_ge(sem, count)


def layernorm_factors(nc, link, x, stats, work, wi, rs, nb, k):
    v, hv, a, y, d, s, m2 = (work[:, k, n:n + 1] for n in range(7))
    n = x.shape[-1]
    link(nc.vector.bn_stats(stats[:, k, :], x))
    even, odd = (stats[:, k, 1:2], stats[:, k, 2:3]), (stats[:, k, 4:5], stats[:, k, 5:6])
    nc.vector.tensor_tensor(d, even[0], odd[0], ALU.subtract)
    nc.vector.tensor_tensor(s, even[0], odd[0], ALU.add)
    link(nc.vector.scalar_tensor_tensor(out=m2, in0=even[1], scalar=n * EPS, in1=odd[1], op0=ALU.add, op1=ALU.add))
    link(nc.vector.scalar_tensor_tensor(out=a, in0=d, scalar=0.25, in1=d, op0=ALU.mult, op1=ALU.mult))
    link(nc.vector.scalar_tensor_tensor(out=v, in0=m2, scalar=1.0 / n, in1=a, op0=ALU.mult, op1=ALU.add))
    nc.vector.tensor_scalar(hv, v, 0.5, None, ALU.mult)
    link(nc.vector.tensor_scalar(wi[:, k, 0:1].bitcast(U32), v.bitcast(U32), 1, None, ALU.logical_shift_right))
    link(nc.vector.tensor_scalar(y.bitcast(I32), wi[:, k, 0:1], -1.0, RSQRT_SEED, ALU.mult, ALU.add))
    for _ in range(NEWTON):
        link(nc.vector.scalar_tensor_tensor(out=a, in0=y, scalar=hv, in1=y, op0=ALU.mult, op1=ALU.mult))
        link(nc.vector.scalar_tensor_tensor(out=y, in0=a, scalar=-1.5, in1=y, op0=ALU.add, op1=ALU.mult))
    link(nc.vector.tensor_scalar(rs, y, XS * (-1.0) ** NEWTON, None, ALU.mult))
    return nc.vector.scalar_tensor_tensor(out=nb, in0=s, scalar=-0.5, in1=rs, op0=ALU.mult, op1=ALU.mult)


def attention_phase(nc, x, ctx_in, g1, wq, wk, wv, wo, bo, x2_dram, ident):
    B, S, D = x.shape
    HD = 64
    KC = D // P
    TT = S // P
    PAIRS = D // P
    HB = 2 * PAIRS
    SC2 = XS * XS
    SHIFT = 44.0
    QS = 1.0 / WS

    xt = x.rearrange("b (t p) d -> b t p d", p=P)
    ct = ctx_in.rearrange("b (t p) d -> b t p d", p=P)
    x2t_d = x2_dram.rearrange("b (t p) d -> b t p d", p=P)

    PRE_UNITS = 4 * TT // 2 + TT + 4 + 1
    BATCH_UNITS = 2 * 9 + 2 * 7
    PRE_HI, BATCH_HI = 2 * TT + TT + 4, 24

    ctx = ExitStack()
    with ctx:
        sb = lambda name, shape, dt=F32: ctx.enter_context(nc.sbuf_tensor(name, shape, dt))
        ps = lambda name, shape, dt=F32: ctx.enter_context(nc.psum_tensor(name, shape, dt))
        sem = lambda name: ctx.enter_context(nc.semaphore(name))

        W = {n: (sb(f"w{n}_hi", [P, KC, D], F16), sb(f"w{n}_lo", [P, KC, D], F16)) for n in "qkvo"}
        x_in = sb("x_in", [P, TT, D])
        c_in = sb("c_in", [P, TT, D])
        xn = sb("xn", [P, 2, D])
        xT = [(sb(f"xT_hi{r}", [P, KC, S], F16), sb(f"xT_lo{r}", [P, KC, S], F16)) for r in range(2)]
        cT = [(sb(f"cT_hi{r}", [P, KC, S], F16), sb(f"cT_lo{r}", [P, KC, S], F16)) for r in range(2)]
        native = {n: (sb(f"{n}_hi", [P, S], F16), sb(f"{n}_lo", [P, S], F16)) for n in "qk"}
        K1, K2, Q1, Q2 = (sb(n, [P, 4, 2, S], F16) for n in ("K1", "K2", "Q1", "Q2"))
        V = sb("V", [P, 2, TT, HB, 2 * HD + 1], F16)
        P32 = sb("P32", [P, TT, S])
        Ph = sb("Ph", [P, 2, TT, S], F16)
        Pl = sb("Pl", [P, 2, TT, S], F16)
        O = [sb(f"O{r}", [P, TT, D]) for r in range(2)]
        oT = (sb("oT_hi", [P, KC, P], F16), sb("oT_lo", [P, KC, P], F16))
        xr = sb("xr", [P, 2, D])
        xb = sb("xb", [P, 2, D])
        x2t = sb("x2t", [P, 2, D])
        tgbo = sb("tgbo", [P, D])
        bo_b = sb("bo_b", [P, D])
        gate = sb("gate1", [P, 3])
        stats = sb("stats", [P, 2, 6])
        work = sb("work", [P, 2, 7])
        wi = sb("wi", [P, 2, 1], I32)
        rs = sb("rs", [P, 2])
        nb = sb("nb", [P, 2])
        mx = sb("mx", [P, 2, TT])
        mneg = sb("mneg", [P, 2 * TT])
        mrow = sb("mrow", [2 * TT, P], F16)
        rec = sb("rec", [P, 2, TT])

        ST = ps("ST", [P, 4, S])
        MX = ps("MX", [P, S])
        PV = ps("PV", [P, 4, P])
        G = ps("G", [P, 2, S])
        stage = {"q": P32, "k": O[0], "v": O[1], "o": P32}

        w_ld = {n: sem(f"w{n}_loaded") for n in "qkvo"}
        w_hi = sem("weight_hi_done")
        w_ready = sem("weights_ready")
        const_ld = sem("constants_loaded")
        tanh_done = sem("gate_tanh_done")
        gate_ready = sem("gate_ready")
        tgbo_ready = sem("gated_bias_ready")
        init_done = sem("pads_written")
        x_ld = [sem(f"x_loaded{t}") for t in range(TT)]
        c_ld = [sem(f"ctx_loaded{t}") for t in range(TT)]
        xr_ld = [sem(f"xr_loaded{r}") for r in range(2)]
        ln_ready = sem("ln_factors_ready")
        xn_ready = sem("xn_ready")
        chain = sem("vector_chain")
        filled = sem("general_bank_filled")
        hi_done = sem("hi_part_written")
        evacuated = sem("general_bank_evacuated")
        qk_dma = [sem(f"qk_arranged{s}") for s in range(4)]
        m_dma = [sem(f"max_rows_placed{s}") for s in range(4)]
        mx_filled = sem("max_scores_filled")
        mx_taken = sem("row_max_taken")
        mneg_ready = sem("negated_max_ready")
        st_filled = sem("scores_filled")
        p_ready = sem("probs_f32_ready")
        ph_ready = sem("probs_hi_ready")
        pl_vec = sem("probs_lo_first_half")
        pl_pool = sem("probs_lo_second_half")
        pv_done = sem("pv_done")
        o_ready = sem("head_output_ready")
        xb_ready = sem("residual_plus_bias_ready")
        x2_st = [sem(f"x2_stored{r}") for r in range(2)]

        QK_DMAS = 12

        def at_batch(unit, b):
            unit.set(b * BATCH_UNITS + (PRE_UNITS - 8), PRE_UNITS - 8)

        def slot_and_use(b, j):
            return j % 4, b + j // 4 + 1

        def batches(eng, unit, step):
            for j in range(4):
                step(0, j)
            with eng.Fori(0, (B - 2) // 2) as i:
                for r in (1, 2):
                    b = i * 2 + r
                    unit(b)
                    for j in range(4):
                        step(b, j, r % 2)
            unit(B - 1)
            for j in range(4):
                step(B - 1, j, (B - 1) % 2)

        block = ctx.enter_context(nc.Block())

        @block.sync
        def _(sp):
            for r in range(2):
                sp.sem_inc(x2_st[r], 16)

            def load_tile(b, t):
                sp.dma_start(x_in[:, t, :], xt[b, t]).then_inc(x_ld[t], 16)
                sp.dma_start(c_in[:, t, :], ct[b, t]).then_inc(c_ld[t], 16)

            def arrange(b, j, uq):
                s, use = slot_and_use(b, j)
                for n, (one, two) in (("q", (Q1, Q2)), ("k", (K1, K2))):
                    sp.wait_ge(evacuated, uq + 1 + (n == "k"))
                    hi, lo = native[n]
                    E, Od = slice(0, HD), slice(HD, P)
                    moves = [(one, E, 0, hi, E), (one, Od, 0, hi if n == "q" else lo, E),
                             (one, Od, 1, hi, Od), (one, E, 1, hi if n == "q" else lo, Od),
                             (two, E, 0, lo if n == "q" else hi, E), (two, Od, 1, lo if n == "q" else hi, Od)]
                    for dst, dp, h, src, sp_ in moves:
                        sp.dma_start(dst[dp, s, h, :], src[sp_, :]).then_inc(qk_dma[s], 16)

            def max_rows(b, j, umt):
                s, use = slot_and_use(b, j)
                sp.wait_ge(evacuated, umt + 1)
                for h, row in ((0, HD), (1, 0)):
                    sp.dma_start(Q2[row:row + 1, s, h, :].rearrange("p (a c) -> p a c", a=TT),
                                 mrow[TT * h:TT * h + TT, :]).then_inc(m_dma[s], 16)

            for t in range(TT):
                load_tile(0, t)
                if t == 0:
                    sp.dma_start(stage["q"][:], wq.rearrange("(c p) n -> p c n", p=P)).then_inc(w_ld["q"], 16)
                    sp.dma_start(stage["k"][:], wk.rearrange("(c p) n -> p c n", p=P)).then_inc(w_ld["k"], 16)
                    sp.dma_start(stage["v"][:], wv.rearrange("(c p) n -> p c n", p=P)).then_inc(w_ld["v"], 16)
            sp.dma_start(bo_b[:], bo.rearrange("(a n) -> a n", a=1).to_broadcast([P, D])).then_inc(const_ld, 16)
            sp.dma_start(gate[:, 0:1], g1.rearrange("(a n) -> a n", a=1).to_broadcast([P, 1])).then_inc(const_ld, 16)
            sp.wait_ge(w_ready, 1)
            sp.dma_start(stage["o"][:], wo.rearrange("(c p) n -> p c n", p=P)).then_inc(w_ld["o"], 16)
            u = 3 * TT
            sp.wait_ge(init_done, 4)
            arrange(0, 0, u)
            arrange(0, 1, u + 2)
            max_rows(0, 0, u + 4)
            unit = Count(PRE_UNITS)

            def step(b, j, r=0):
                known = isinstance(b, int)
                more = not known or b < B - 1
                if j == 0 and more:
                    for t in range(TT):
                        load_tile(b + 1, t)
                uq = unit.take() if more or j < 2 else None
                uk = unit.take() if more or j < 2 else None
                w = not known or b > 0
                if w:
                    since(sp, x2_st[j % 2], (b * 2 - 1 + j // 2) * 16)
                    sp.dma_start(xr[:, j % 2, :], xt[b - 1, j]).then_inc(xr_ld[j % 2], 16)
                if uq is not None:
                    arrange(b, j + 2, uq)
                if w:
                    unit.take()
                if more:
                    unit.take(2 if j < 2 else 1)
                umt = unit.take() if more or j < 3 else None
                if umt is not None:
                    max_rows(b, j + 1, umt)
                if w:
                    sp.wait_ge(evacuated, unit.take() + 1)
                    sp.dma_start(x2t_d[b - 1, j], x2t[:, j % 2, :]).then_inc(x2_st[j % 2], 16)
                if more:
                    unit.take(2 if j < 2 else 1)

            batches(sp, lambda b: at_batch(unit, b), step)
            for j in range(4):
                sp.wait_ge(x2_st[j % 2], (B * 2 - 1 + j // 2) * 16)
                sp.dma_start(xr[:, j % 2, :], xt[B - 1, j]).then_inc(xr_ld[j % 2], 16)
                unit.take()
                sp.wait_ge(evacuated, unit.take() + 1)
                sp.dma_start(x2t_d[B - 1, j], x2t[:, j % 2, :]).then_inc(x2_st[j % 2], 16)
            for r in range(2):
                sp.wait_ge(x2_st[r], (B * 2 + 1) * 16)

        @block.gpsimd
        def _(pool):
            pool.wait_ge(tanh_done, 1)
            nc.gpsimd.tensor_scalar(tgbo[:], bo_b[:], gate[:, 1:2], None, ALU.mult).then_inc(tgbo_ready, 1)
            pool.wait_ge(tgbo_ready, 1)

            def step(b, j, r=0):
                known = isinstance(b, int)
                if not known or b > 0:
                    k = j % 2
                    pool.wait_ge(xr_ld[k], (b * 2 - 1 + j // 2) * 16)
                    since(pool, x2_st[k], (b * 2 - 1 + j // 2) * 16)
                    nc.gpsimd.tensor_tensor(xb[:, k, :], xr[:, k, :], tgbo[:], ALU.add).then_inc(xb_ready, 1)
                for hh in range(2):
                    hd = b * HB + 2 * j + hh
                    pool.wait_ge(ph_ready, hd * 2 + 2)
                    nc.gpsimd.tensor_tensor(Pl[:, hh, 2:4, :], P32[:, 2:4, :], Ph[:, hh, 2:4, :],
                                            ALU.subtract).then_inc(pl_pool, 1)

            batches(pool, lambda b: None, step)
            for j in range(4):
                k = j % 2
                pool.wait_ge(xr_ld[k], (B * 2 - 1 + j // 2) * 16)
                pool.wait_ge(x2_st[k], (B * 2 - 1 + j // 2) * 16)
                nc.gpsimd.tensor_tensor(xb[:, k, :], xr[:, k, :], tgbo[:], ALU.add).then_inc(xb_ready, 1)

        @block.scalar
        def _(act):
            def hi_part(u, dst, scale):
                act.wait_ge(filled, u + 1)
                src = G[:, unit.bank, :]
                if dst.shape[-1] != S:
                    src = src.rearrange("p (c n) -> p c n", c=dst.shape[1])
                nc.scalar.activation(dst, src, ACT.Copy, scale=scale).then_inc(hi_done, 1)

            def normalise(n, t):
                act.wait_ge(ln_ready, n + 1)
                nc.scalar.activation(xn[:, t % 2, :], x_in[:, t, :], ACT.Identity,
                                     scale=rs[:, t % 2:t % 2 + 1], bias=nb[:, t % 2:t % 2 + 1]).then_inc(xn_ready, 1)

            def v_view(r, t, lo):
                return V[:, r, t, :, (HD + 1 if lo else 0):(2 * HD + 1 if lo else HD)]

            def exps(b, j, hh):
                hd = b * HB + 2 * j + hh
                for half in range(2):
                    cs = slice(2 * half, 2 * half + 2)
                    act.wait_ge(st_filled, hd * 2 + half + 1)
                    since(act, pl_pool if half else pl_vec, hd)
                    nc.scalar.activation(P32[:, cs, :], ST[:, cs, :], ACT.Exp,
                                         scale=0.125 / SC2).then_inc(p_ready, 1)
                    since(act, pv_done, hd - 1)
                    nc.scalar.activation(Ph[:, hh, cs, :], ST[:, cs, :], ACT.Exp,
                                         scale=0.125 / SC2).then_inc(ph_ready, 1)

            def weight_hi(n):
                act.wait_ge(w_ld[n], 16)
                nc.scalar.activation(W[n][0][:], stage[n][:], ACT.Copy, scale=WS).then_inc(w_hi, 1)

            weight_hi("q")
            weight_hi("k")
            unit = Count(0)

            def transposed(b, t, r):
                for dst, scale in ((xT[r][0], 1.0), (cT[r][0], XS)):
                    hi_part(unit.take(), dst[:, :, t * P:(t + 1) * P], scale)

            for t in range(TT):
                normalise(t, t)
                transposed(0, t, 0)
            weight_hi("v")
            weight_hi("o")
            act.wait_ge(const_ld, 32)
            nc.scalar.activation(gate[:, 1:2], gate[:, 0:1], ACT.Tanh).then_inc(tanh_done, 1)
            for t in range(TT):
                u = unit.take()
                act.wait_ge(filled, u + 1)
                nc.scalar.activation(v_view(0, t, False), G[:, unit.bank, :].rearrange("p (h d) -> p h d", d=HD),
                                     ACT.Copy, scale=QS).then_inc(hi_done, 1)
            for pair in range(2):
                for n in "qk":
                    if pair:
                        act.wait_ge(qk_dma[0], QK_DMAS * 16)
                    hi_part(unit.take(), native[n][0][:], QS)
            unit.take()

            def step(b, j, r=0):
                known = isinstance(b, int)
                more = not known or b < B - 1
                w = not known or b > 0
                nr = 1 - r
                if more and j < 2:
                    normalise(b * 4 + 4 + 2 * j, 2 * j)
                exps(b, j, 0)
                if more or j < 2:
                    s, use = slot_and_use(b, j + 1)
                    for n in "qk":
                        act.wait_ge(qk_dma[s], use * QK_DMAS * 16)
                        hi_part(unit.take(), native[n][0][:], QS)
                if more and j < 2:
                    normalise(b * 4 + 5 + 2 * j, 2 * j + 1)
                exps(b, j, 1)
                if w:
                    hi_part(unit.take(), oT[0][:], 1.0)

                def side(t):
                    if j < 2:
                        transposed(b, t, nr)
                    else:
                        u = unit.take()
                        act.wait_ge(filled, u + 1)
                        nc.scalar.activation(v_view(nr, t, False), G[:, unit.bank, :].rearrange("p (h d) -> p h d", d=HD),
                                             ACT.Copy, scale=QS).then_inc(hi_done, 1)
                if more:
                    side(2 * (j % 2))
                if more or j < 3:
                    unit.take()
                if w:
                    unit.take()
                if more:
                    side(2 * (j % 2) + 1)

            batches(act, lambda b: at_batch(unit, b), step)
            for j in range(4):
                hi_part(unit.take(), oT[0][:], 1.0)
                unit.take()

        @block.vector
        def _(dve):
            links = Count(0)

            def link(ins):
                ins.then_inc(chain, 1)
                dve.wait_ge(chain, links.take() + 1)

            unit = Count(0)
            hi = Count(0)

            def lo_part(dst, hi_view, scale):
                u = unit.take()
                dve.wait_ge(hi_done, hi.take() + 1)
                src = G[:, unit.bank, :]
                if dst.shape[-1] != S:
                    src = src.rearrange("p (c n) -> p c n", c=dst.shape[1])
                nc.vector.scalar_tensor_tensor(out=dst, in0=src, scalar=scale, in1=hi_view,
                                               op0=ALU.mult, op1=ALU.subtract).then_inc(evacuated, 1)

            def factors(n, t, use):
                dve.wait_ge(x_ld[t], use * 16)
                k = t % 2
                layernorm_factors(nc, link, x_in[:, t, :], stats, work, wi,
                                  rs[:, k:k + 1], nb[:, k:k + 1], k).then_inc(ln_ready, 1)

            def row_max(n, k):
                dve.wait_ge(mx_filled, n + 1)
                nc.vector.tensor_reduce(out=mx[:, k // TT, k % TT:k % TT + 1], in_=MX[:], axis=AXX,
                                        op=ALU.max).then_inc(mx_taken, 1)

            def negate(n):
                dve.wait_ge(mx_taken, n)
                nc.vector.tensor_scalar(mneg[:], mx[:].rearrange("p h t -> p (h t)"), -1.0 / SC2, SHIFT,
                                        ALU.mult, ALU.add).then_inc(mneg_ready, 1)

            def max_rows():
                u = unit.take()
                dve.wait_ge(filled, u + 1)
                nc.vector.tensor_copy(mrow[:], G[0:2 * TT, unit.bank, 0:P]).then_inc(evacuated, 1)

            def transposed(t, r):
                for (hi_t, lo_t), scale in ((xT[r], 1.0), (cT[r], XS)):
                    c = slice(t * P, (t + 1) * P)
                    lo_part(lo_t[:, :, c], hi_t[:, :, c], scale)

            def v_lo(t, r):
                u = unit.take()
                dve.wait_ge(hi_done, hi.take() + 1)
                nc.vector.scalar_tensor_tensor(
                    out=V[:, r, t, :, HD + 1:], in0=G[:, unit.bank, :].rearrange("p (h d) -> p h d", d=HD), scalar=QS,
                    in1=V[:, r, t, :, 0:HD], op0=ALU.mult, op1=ALU.subtract).then_inc(evacuated, 1)

            def head_out(hd, j, hh, r):
                dve.wait_ge(pv_done, hd + 1)
                link(nc.vector.reciprocal(rec[:, hh, :], PV[:, :, HD:HD + 1].rearrange("p t o -> p (t o)")))
                h = 2 * j + hh
                nc.vector.tensor_tensor(O[r][:, :, h * HD:(h + 1) * HD], PV[:, :, 0:HD],
                                        rec[:, hh, :].unsqueeze(2).to_broadcast([P, TT, HD]),
                                        ALU.mult).then_inc(o_ready, 1)

            def probs_lo(hd, hh):
                dve.wait_ge(ph_ready, hd * 2 + 1)
                nc.vector.tensor_tensor(Pl[:, hh, 0:2, :], P32[:, 0:2, :], Ph[:, hh, 0:2, :],
                                        ALU.subtract).then_inc(pl_vec, 1)

            def x2_rows(w, j, uses):
                u = unit.take()
                dve.wait_ge(filled, u + 1)
                dve.wait_ge(xb_ready, w + 1)
                since(dve, x2_st[j % 2], uses)
                nc.vector.scalar_tensor_tensor(out=x2t[:, j % 2, :], in0=G[:, unit.bank, :], scalar=gate[:, 2:3],
                                               in1=xb[:, j % 2, :], op0=ALU.mult, op1=ALU.add).then_inc(evacuated, 1)

            def weight_lo(n, k):
                dve.wait_ge(w_hi, k + 1)
                nc.vector.scalar_tensor_tensor(out=W[n][1][:].rearrange("p c n -> p (c n)"),
                                               in0=stage[n][:].rearrange("p c n -> p (c n)"), scalar=WS,
                                               in1=W[n][0][:].rearrange("p c n -> p (c n)"),
                                               op0=ALU.mult, op1=ALU.subtract).then_inc(w_ready, 1)

            for t in range(2):
                factors(t, t, 1)
            for h, dp in ((0, slice(HD, P)), (1, slice(0, HD))):
                nc.vector.memset(K2[dp, :, h, :], 0.0).then_inc(init_done, 1)
                nc.vector.memset(Q2[dp, :, h, :], 0.0).then_inc(init_done, 1)
            dve.wait_ge(init_done, 4)
            for h, row in ((0, HD), (1, 0)):
                nc.vector.memset(K2[row:row + 1, :, h, :], SC2).then_inc(init_done, 1)
            nc.vector.memset(V[:, :, :, :, HD:HD + 1], 1.0).then_inc(init_done, 1)
            weight_lo("q", 0)
            weight_lo("k", 1)
            for t in range(TT):
                transposed(t, 0)
                if t < 2:
                    dve.wait_ge(xn_ready, t + 1)
                    factors(t + 2, t + 2, 1)
            weight_lo("v", 2)
            weight_lo("o", 3)
            dve.wait_ge(tanh_done, 1)
            nc.vector.tensor_scalar(gate[:, 2:3], gate[:, 1:2], 1.0 / (XS * WS), None, ALU.mult).then_inc(gate_ready, 1)
            dve.wait_ge(gate_ready, 1)
            for t in range(TT):
                v_lo(t, 0)
            for pair in range(2):
                for n in "qk":
                    lo_part(native[n][1][:], native[n][0][:], QS)
            for k in range(8):
                row_max(k, k)
            negate(8)
            max_rows()

            def step(b, j, r=0):
                known = isinstance(b, int)
                more = not known or b < B - 1
                w = not known or b > 0
                nr = 1 - r
                hd = b * HB + 2 * j
                mxn = b * 32 + 8 * (j + 1)
                nmax = more or j < 3

                def maxima(*ks):
                    for k in ks:
                        if nmax:
                            row_max(mxn + k, k)

                def side(t):
                    transposed(t, nr) if j < 2 else v_lo(t, nr)

                def proj_lo(n):
                    if more or j < 2:
                        lo_part(native[n][1][:], native[n][0][:], QS)

                if more and j < 2:
                    dve.wait_ge(xn_ready, b * 4 + 2 * j + 3)
                    factors(0, 2 * j, b + 2)
                maxima(0, 1)
                proj_lo("q")
                maxima(2)
                if w or j:
                    pj = (j - 1) % 4
                    head_out(hd - 1, pj, 1, r if j else nr)
                maxima(3)
                probs_lo(hd, 0)
                maxima(4)
                proj_lo("k")
                if more and j < 2:
                    dve.wait_ge(xn_ready, b * 4 + 2 * j + 4)
                    factors(0, 2 * j + 1, b + 2)
                maxima(5, 6)
                if w:
                    lo_part(oT[1][:], oT[0][:], 1.0)
                maxima(7)
                if nmax:
                    negate(mxn + 8)
                if more:
                    side(2 * (j % 2))
                if nmax:
                    max_rows()
                if w:
                    x2_rows(b * 4 - 4 + j, j, (b * 2 - 1 + j // 2) * 16)
                probs_lo(hd + 1, 1)
                head_out(hd, j, 0, r)
                if more:
                    side(2 * (j % 2) + 1)

            def at_counts(b):
                at_batch(unit, b)
                hi.value = b * BATCH_HI + (PRE_HI - 4)
                links.value = b * (HB + TT * LN_CHAIN) + (TT * LN_CHAIN - 1)

            batches(dve, at_counts, step)
            head_out(B * HB - 1, 3, 1, (B - 1) % 2)
            for j in range(4):
                lo_part(oT[1][:], oT[0][:], 1.0)
                x2_rows(B * 4 - 4 + j, j, (B * 2 - 1 + j // 2) * 16)

        @block.tensor
        def _(pe):
            unit = Count(0)

            def bank():
                u = unit.take()
                since(pe, evacuated, u - 1)
                return u, G[:, unit.bank, :]

            def product(out, parts, n0=0, n1=None):
                n1 = len(parts) if n1 is None else n1
                for n in range(n0, n1):
                    a, m = parts[n]
                    last = nc.tensor.matmul(out, a, m, start=(n == 0), stop=(n == len(parts) - 1))
                return last

            def split_parts(stat, mov):
                return [(stat(a, c), mov(m, c)) for c in range(KC) for a, m in ((0, 0), (0, 1), (1, 0))]

            def transposes(src):
                u, g = bank()
                for c in range(KC):
                    last = nc.tensor.transpose(g[:, c * P:(c + 1) * P], src[:, c * P:(c + 1) * P], ident[:])
                last.then_inc(filled, 1)

            def x_tile(t, n):
                pe.wait_ge(xn_ready, n + 1)
                transposes(xn[:, t % 2, :])

            def c_tile(t, use):
                pe.wait_ge(c_ld[t], use * 16)
                transposes(c_in[:, t, :])

            def qk_parts(n, pair, r):
                act_t = xT[r] if n == "q" else cT[r]
                return split_parts(lambda a, c: W[n][a][:, c, pair * P:(pair + 1) * P],
                                   lambda m, c: act_t[m][:, c, :])

            def v_parts(t, r):
                return split_parts(lambda a, c: cT[r][a][:, c, t * P:(t + 1) * P], lambda m, c: W["v"][m][:, c, :])

            def row_max_scores(n, k, s, use):
                h, t = k // TT, k % TT
                if k == 0:
                    pe.wait_ge(qk_dma[s], use * QK_DMAS * 16)
                since(pe, mx_taken, n)
                nc.tensor.matmul(MX[:], Q1[:, s, h, t * P:(t + 1) * P], K1[:, s, h, :],
                                 start=True, stop=True).then_inc(mx_filled, 1)

            def max_transpose(pairs_before):
                u, g = bank()
                pe.wait_ge(mneg_ready, pairs_before + 1)
                nc.tensor.transpose(g[0:2 * TT, 0:P], mneg[:], ident[:]).then_inc(filled, 1)

            def scores(b, j, hh):
                hd = b * HB + 2 * j + hh
                if hh == 0:
                    pe.wait_ge(m_dma[j], (b + 1) * 32)
                for half in range(2):
                    since(pe, ph_ready, hd * 2 + half - 1)
                    for c in (2 * half, 2 * half + 1):
                        cols = slice(c * P, (c + 1) * P)
                        nc.tensor.matmul(ST[:, c, :], K1[:, j, hh, cols], Q1[:, j, hh, :], start=True, stop=False)
                        last = nc.tensor.matmul(ST[:, c, :], K2[:, j, hh, cols], Q2[:, j, hh, :],
                                                start=False, stop=True)
                    last.then_inc(st_filled, 1)

            def weighted(hd, h, r):
                hh = h % 2
                pe.wait_ge(pl_vec, hd + 1)
                pe.wait_ge(pl_pool, hd + 1)
                since(pe, o_ready, hd)
                for t in range(TT):
                    cols = slice(t * P, (t + 1) * P)
                    for c in range(TT):
                        nc.tensor.matmul(PV[:, t, 0:HD + 1], Ph[:, hh, c, cols], V[:, r, c, h, 0:HD + 1],
                                         start=(c == 0), stop=False)
                        nc.tensor.matmul(PV[:, t, 0:HD], Ph[:, hh, c, cols], V[:, r, c, h, HD + 1:],
                                         start=False, stop=False)
                        last = nc.tensor.matmul(PV[:, t, 0:HD + 1], Pl[:, hh, c, cols], V[:, r, c, h, 0:HD + 1],
                                                start=False, stop=(c == TT - 1))
                last.then_inc(pv_done, 1)

            def out_project(split):
                u, g = bank()
                pe.wait_ge(evacuated, split + 1)
                product(g, split_parts(lambda a, c: oT[a][:, c, :],
                                       lambda m, c: W["o"][m][:, c, :])).then_inc(filled, 1)

            for t in range(TT):
                x_tile(t, t)
                c_tile(t, 1)
            pe.wait_ge(w_ready, 3)
            pe.wait_ge(evacuated, 2 * TT)
            for t in range(TT):
                u, g = bank()
                product(g, v_parts(t, 0)).then_inc(filled, 1)
            for pair in range(2):
                for n in "qk":
                    u, g = bank()
                    product(g, qk_parts(n, pair, 0)).then_inc(filled, 1)
            for k in range(8):
                row_max_scores(k, k, 0, 1)
            max_transpose(0)
            pe.wait_ge(init_done, 7)
            pe.wait_ge(w_ready, 4)

            def step(b, j, r=0):
                known = isinstance(b, int)
                more = not known or b < B - 1
                w = not known or b > 0
                nr = 1 - r
                hd = b * HB + 2 * j
                mxn = b * 32 + 8 * (j + 1)
                s, use = slot_and_use(b, j + 1)
                qk_r = r if j < 2 else nr

                def maxima(*ks):
                    for k in ks:
                        if more or j < 3:
                            row_max_scores(mxn + k, k, s, use)

                def project(n, ks):
                    if more or j < 2:
                        u, g = bank()
                        if j == 2 and n == "q":
                            pe.wait_ge(evacuated, u)
                        parts = qk_parts(n, (j + 2) % 4, qk_r)
                        product(g, parts, 0, 6)
                        maxima(ks)
                        product(g, parts, 6).then_inc(filled, 1)
                    else:
                        maxima(ks)

                def side(t):
                    if j < 2:
                        x_tile(t, b * 4 + 4 + t)
                        c_tile(t, b + 2)
                    else:
                        u, g = bank()
                        product(g, v_parts(t, nr)).then_inc(filled, 1)

                scores(b, j, 0)
                maxima(0)
                project("q", 1)
                maxima(2)
                if w or j:
                    weighted(hd - 1, (2 * j - 1) % HB, r if j else nr)
                maxima(3)
                project("k", 4)
                maxima(5)
                scores(b, j, 1)
                maxima(6)
                if w:
                    pe.wait_ge(o_ready, b * HB)
                    split = unit.value
                    transposes(O[nr][:, j, :])
                maxima(7)
                if more:
                    side(2 * (j % 2))
                if more or j < 3:
                    max_transpose(b * 4 + j + 1)
                if w:
                    out_project(split)
                weighted(hd, 2 * j, r)
                if more:
                    side(2 * (j % 2) + 1)

            batches(pe, lambda b: at_batch(unit, b), step)
            weighted(B * HB - 1, HB - 1, (B - 1) % 2)
            pe.wait_ge(o_ready, B * HB)
            for j in range(4):
                split = unit.value
                transposes(O[(B - 1) % 2][:, j, :])
                out_project(split)


def ffn_phase(nc, x2_dram, g2, gate_w, wu, wv, wo, out, ident):
    T_ALL = x2_dram.shape[0] * x2_dram.shape[1]
    D = x2_dram.shape[2]
    E, _, R = wu.shape
    KC = D // P
    ER = E * R
    HALF = ER // 2
    NH = HALF // P
    TILES = T_ALL // P
    x2_d = x2_dram.rearrange("b s d -> (b s) d").rearrange("(t p) d -> t p d", p=P)
    out_d = out.rearrange("b s d -> (b s) d").rearrange("(t p) d -> t p d", p=P)

    ctx = ExitStack()
    with ctx:
        sb = lambda name, shape, dt=F32: ctx.enter_context(nc.sbuf_tensor(name, shape, dt))
        ps = lambda name, shape, dt=F32: ctx.enter_context(nc.psum_tensor(name, shape, dt))
        sem = lambda name: ctx.enter_context(nc.semaphore(name))
        stage = {n: sb(f"f{n}_stage", [P, KC * ER]) for n in "uvo"}
        g_stage = sb("gate_w_stage", [P, KC * E])
        W = {n: (sb(f"f{n}_hi", [P, KC * ER], F16), sb(f"f{n}_lo", [P, KC * ER], F16)) for n in "uvo"}
        Wg = (sb("fg_hi", [P, KC, E], F16), sb("fg_lo", [P, KC, E], F16))
        x2s = sb("x2s", [P, 2, D])
        xn = sb("xn2", [P, 2, D])
        xT = (sb("x2T_hi", [P, 2, KC, P], F16), sb("x2T_lo", [P, 2, KC, P], F16))
        th = sb("th", [P, 2, HALF])
        a_sb = sb("a_sb", [P, 2, HALF])
        sw = sb("sw", [P, 2, HALF])
        sT = (sb("sT_hi", [P, 2, NH, P], F16), sb("sT_lo", [P, 2, NH, P], F16))
        res = sb("res", [P, 2, D])
        stats = sb("stats2", [P, 2, 6])
        work = sb("work2", [P, 2, 7])
        wi = sb("wi2", [P, 2, 1], I32)
        rs = sb("rs2", [P, 2])
        nb = sb("nb2", [P, 2])
        lg = sb("lg", [P, 2, E])
        top = sb("top", [P, 2, 8])
        took = sb("took", [P, 1])
        idx = sb("idx", [P, 2, 8], U32)
        idf = sb("idf", [P, 2, 2])
        df = sb("df", [P, 2, 4])
        cw = sb("cw", [P, 2, 2, E])
        iota = sb("iota", [P, E])
        gate = sb("gate2", [P, 3])

        U = ps("U", [P, 2, HALF])
        Vp = ps("Vp", [P, 2, HALF])
        TR = ps("TR", [P, D])
        TS = ps("TS", [P, HALF])
        L = ps("L", [P, E])
        Y = ps("Y", [P, D])

        w_ld = {n: sem(f"f{n}_loaded") for n in "uvog"}
        const_ld = sem("f_constants_loaded")
        iota_done = sem("iota_done")
        tanh_done, gate_ready = sem("f_tanh_done"), sem("f_gate_ready")
        w_hi, w_ready = sem("f_weight_hi"), sem("f_weights_ready")
        x_ld = [sem(f"x2_loaded{r}") for r in range(2)]
        st = [sem(f"out_stored{r}") for r in range(2)]
        chain = sem("f_vector_chain")
        ln_ready, xn_ready = sem("f_ln_ready"), sem("f_xn_ready")
        tr_filled, tr_hi, tr_lo = sem("x2_transposed"), sem("x2T_hi_written"), sem("x2T_lo_written")
        lg_filled, diff_ready, exp_ready, cw_ready = (sem("logits_filled"), sem("logit_gap_ready"),
                                                      sem("gap_exp_ready"), sem("weights_of_experts_ready"))
        uv_filled, tanh_ready, s_ready = sem("uv_filled"), sem("tanh_ready"), sem("s_ready")
        ts_filled, s_hi, s_lo = sem("s_transposed"), sem("sT_hi_written"), sem("sT_lo_written")
        y_filled, out_ready = sem("y_filled"), sem("out_ready")
        block = ctx.enter_context(nc.Block())

        @block.sync
        def _(sp):
            sp.dma_start(x2s[:, 0, :], x2_d[0]).then_inc(x_ld[0], 16)
            sp.dma_start(g_stage[:].rearrange("p (c e) -> p c e", c=KC),
                         gate_w.rearrange("(c p) e -> p c e", p=P)).then_inc(w_ld["g"], 16)
            for n, w in (("u", wu), ("v", wv)):
                for c in range(KC):
                    sp.dma_start(stage[n][:, c * ER:(c + 1) * ER].rearrange("p (e r) -> p e r", e=E),
                                 w.rearrange("e (c p) r -> c p e r", p=P)[c]).then_inc(w_ld[n], 16)
            sp.dma_start(stage["o"][:].rearrange("p (e n) -> p e n", e=E), wo.rearrange("e r n -> r e n")).then_inc(w_ld["o"], 16)
            sp.dma_start(gate[:, 0:1], g2.rearrange("(a n) -> a n", a=1).to_broadcast([P, 1])).then_inc(const_ld, 16)
            sp.dma_start(x2s[:, 1, :], x2_d[1]).then_inc(x_ld[1], 16)

            def step(t, r, more):
                sp.wait_ge(out_ready, t + 1)
                sp.dma_start(out_d[t], res[:, r, :]).then_inc(st[r], 16)
                if more:
                    sp.dma_start(x2s[:, r, :], x2_d[t + 2]).then_inc(x_ld[r], 16)

            for r in range(2):
                step(r, r, True)
            with sp.Fori(1, TILES // 2 - 1) as i:
                for r in range(2):
                    step(i * 2 + r, r, True)
            for r in range(2):
                step(TILES - 2 + r, r, False)
            for r in range(2):
                sp.wait_ge(st[r], TILES // 2 * 16)

        @block.gpsimd
        def _(pool):
            nc.gpsimd.iota(iota[:], [[1, E]], base=0, channel_multiplier=0,
                           allow_small_or_imprecise_dtypes=True).then_inc(iota_done, 1)

        @block.scalar
        def _(act):
            def front(t, r):
                act.wait_ge(ln_ready, t + 1)
                nc.scalar.activation(xn[:, r, :], x2s[:, r, :], ACT.Identity, scale=rs[:, r:r + 1],
                                     bias=nb[:, r:r + 1]).then_inc(xn_ready, 1)
                act.wait_ge(tr_filled, t + 1)
                nc.scalar.activation(xT[0][:, r].rearrange("p c n -> p (c n)"), TR[:], ACT.Copy).then_inc(tr_hi, 1)
                act.wait_ge(diff_ready, t + 1)
                nc.scalar.activation(df[:, r, 1:2], df[:, r, 0:1], ACT.Exp).then_inc(exp_ready, 1)

            def experts(t, r, h):
                n = t * 2 + h
                act.wait_ge(uv_filled, n + 1)
                nc.scalar.activation(th[:, h, :], U[:, h, :], ACT.Tanh, scale=0.5 / (XS * WS)).then_inc(tanh_ready, 1)
                act.wait_ge(ts_filled, n + 1)
                nc.scalar.activation(sT[0][:, h].rearrange("p c n -> p (c n)"), TS[:], ACT.Copy).then_inc(s_hi, 1)

            def weight_hi(n, dst):
                act.wait_ge(w_ld[n], 16 * (KC if n in "uv" else 1))
                nc.scalar.activation(dst, (g_stage if n == "g" else stage[n])[:], ACT.Copy, scale=WS).then_inc(w_hi, 1)

            weight_hi("g", Wg[0][:].rearrange("p c e -> p (c e)"))
            act.wait_ge(const_ld, 16)
            nc.scalar.activation(gate[:, 1:2], gate[:, 0:1], ACT.Tanh).then_inc(tanh_done, 1)
            for n in "uvo":
                weight_hi(n, W[n][0][:])
            front(0, 0)

            def step(t, r, more):
                experts(t, r, 0)
                if more:
                    front(t + 1, 1 - r)
                experts(t, r, 1)

            for r in range(2):
                step(r, r, True)
            with act.Fori(1, TILES // 2 - 1) as i:
                for r in range(2):
                    step(i * 2 + r, r, True)
            step(TILES - 2, 0, True)
            step(TILES - 1, 1, False)

        @block.vector
        def _(dve):
            links = Count(0)

            def link(ins):
                ins.then_inc(chain, 1)
                dve.wait_ge(chain, links.take() + 1)

            def weight_lo(k, src, hi, lo):
                dve.wait_ge(w_hi, k + 1)
                nc.vector.scalar_tensor_tensor(out=lo, in0=src, scalar=WS, in1=hi, op0=ALU.mult,
                                               op1=ALU.subtract).then_inc(w_ready, 1)

            def front(t, r, use):
                dve.wait_ge(x_ld[r], use * 16)
                layernorm_factors(nc, link, x2s[:, r, :], stats, work, wi, rs[:, r:r + 1], nb[:, r:r + 1],
                                  r).then_inc(ln_ready, 1)
                dve.wait_ge(tr_hi, t + 1)
                flat = lambda z: z.rearrange("p c n -> p (c n)")
                nc.vector.tensor_tensor(flat(xT[1][:, r]), TR[:], flat(xT[0][:, r]), ALU.subtract).then_inc(tr_lo, 1)
                dve.wait_ge(lg_filled, t + 1)
                link(nc.vector.tensor_scalar(lg[:, r, :], L[:], 1.0 / (XS * WS), None, ALU.mult))
                nc.vector.tensor_copy(took[:], lg[:, r, 0:1])
                link(nc.vector.max(top[:, r, :], lg[:, r, :]))
                nc.vector.tensor_tensor(df[:, r, 0:1], top[:, r, 1:2], top[:, r, 0:1], ALU.subtract).then_inc(diff_ready, 1)
                link(nc.vector.max_index(idx[:, r, :], top[:, r, :], lg[:, r, :]))
                link(nc.vector.tensor_copy(idf[:, r, :], idx[:, r, 0:2]))
                dve.wait_ge(exp_ready, t + 1)
                link(nc.vector.tensor_scalar(df[:, r, 3:4], df[:, r, 1:2], 1.0, None, ALU.add))
                link(nc.vector.reciprocal(df[:, r, 2:3], df[:, r, 3:4]))
                link(nc.vector.tensor_tensor(df[:, r, 3:4], df[:, r, 1:2], df[:, r, 2:3], ALU.mult))
                for k in range(2):
                    last = nc.vector.tensor_scalar(cw[:, r, k, :], iota[:], idf[:, r, k:k + 1], df[:, r, 2 + k:3 + k],
                                                   ALU.is_equal, ALU.mult)
                link(last)
                link(nc.vector.tensor_tensor(cw[:, r, 0, :], cw[:, r, 0, :], cw[:, r, 1, :], ALU.add))
                nc.vector.tensor_scalar(cw[:, r, 1, :], cw[:, r, 0, :], XS * 0.5 / (XS * WS) ** 2, None,
                                        ALU.mult).then_inc(cw_ready, 1)

            def product(t, r, h):
                n = t * 2 + h
                dve.wait_ge(tanh_ready, n + 1)
                link(nc.vector.scalar_tensor_tensor(out=a_sb[:, h, :], in0=th[:, h, :], scalar=1.0, in1=U[:, h, :],
                                                    op0=ALU.add, op1=ALU.mult))
                dve.wait_ge(cw_ready, t + 1)
                for e in range(NH):
                    cols = slice(e * P, (e + 1) * P)
                    last = nc.vector.scalar_tensor_tensor(
                        out=sw[:, h, cols], in0=a_sb[:, h, cols], scalar=cw[:, r, 1, h * NH + e:h * NH + e + 1],
                        in1=Vp[:, h, cols], op0=ALU.mult, op1=ALU.mult)
                last.then_inc(s_ready, 1)

            def product_lo(n, h):
                dve.wait_ge(s_hi, n + 1)
                flat = lambda z: z.rearrange("p c n -> p (c n)")
                nc.vector.tensor_tensor(flat(sT[1][:, h]), TS[:], flat(sT[0][:, h]), ALU.subtract).then_inc(s_lo, 1)

            weight_lo(0, g_stage[:], Wg[0][:].rearrange("p c e -> p (c e)"), Wg[1][:].rearrange("p c e -> p (c e)"))
            for k, n in enumerate("uvo"):
                weight_lo(k + 1, stage[n][:], W[n][0][:], W[n][1][:])
            dve.wait_ge(tanh_done, 1)
            nc.vector.tensor_scalar(gate[:, 2:3], gate[:, 1:2], 1.0 / (XS * WS), None, ALU.mult).then_inc(gate_ready, 1)
            dve.wait_ge(gate_ready, 1)
            dve.wait_ge(iota_done, 1)
            front(0, 0, 1)
            FRONT = links.value
            STEP = FRONT + 2

            def step(t, r, use, more, stored):
                product(t, r, 0)
                product_lo(t * 2, 0)
                if more:
                    front(t + 1, 1 - r, use)
                product(t, r, 1)
                product_lo(t * 2 + 1, 1)
                dve.wait_ge(y_filled, t + 1)
                since(dve, st[r], stored * 16)
                nc.vector.scalar_tensor_tensor(out=res[:, r, :], in0=Y[:], scalar=gate[:, 2:3], in1=x2s[:, r, :],
                                               op0=ALU.mult, op1=ALU.add).then_inc(out_ready, 1)

            for r in range(2):
                links.set(FRONT + r * STEP, 0)
                step(r, r, 1 + r, True, 0)
            with dve.Fori(1, TILES // 2 - 1) as i:
                for r in range(2):
                    links.set(i * (2 * STEP) + (FRONT + r * STEP), 0)
                    step(i * 2 + r, r, i + (1 + r), True, i)
            links.set((TILES - 2) * STEP + FRONT, 0)
            step(TILES - 2, 0, TILES // 2, True, TILES // 2 - 1)
            step(TILES - 1, 1, 0, False, TILES // 2 - 1)

        @block.tensor
        def _(pe):
            def split(out, stat, mov, chunks, start=True, stop=True, exact=False):
                parts = [(stat(a, c), mov(m, c)) for c in range(chunks)
                         for a, m in ((0, 0), (0, 1), (1, 0)) + (((1, 1),) if exact else ())]
                for n, (a, m) in enumerate(parts):
                    last = nc.tensor.matmul(out, a, m, start=start and n == 0, stop=stop and n == len(parts) - 1)
                return last

            def front(t, r):
                pe.wait_ge(xn_ready, t + 1)
                since(pe, tr_lo, t)
                for c in range(KC):
                    last = nc.tensor.transpose(TR[:, c * P:(c + 1) * P], xn[:, r, c * P:(c + 1) * P], ident[:])
                last.then_inc(tr_filled, 1)

            def logits(t, r):
                pe.wait_ge(tr_lo, t + 1)
                since(pe, cw_ready, t)
                split(L[:], lambda a, c: xT[a][:, r, c, :], lambda m, c: Wg[m][:, c, :], KC,
                      exact=True).then_inc(lg_filled, 1)

            def up(t, r, h):
                since(pe, s_ready, (t - 1) * 2 + h + 1)
                for n, dst in (("u", U), ("v", Vp)):
                    last = split(dst[:, h, :], lambda a, c: xT[a][:, r, c, :],
                                 lambda m, c: W[n][m][:, c * ER + h * HALF:c * ER + (h + 1) * HALF], KC)
                last.then_inc(uv_filled, 1)

            def s_transposes(n, h):
                pe.wait_ge(s_ready, n + 1)
                since(pe, s_lo, n)
                for c in range(NH):
                    last = nc.tensor.transpose(TS[:, c * P:(c + 1) * P], sw[:, h, c * P:(c + 1) * P], ident[:])
                last.then_inc(ts_filled, 1)

            def down(n, t, h):
                pe.wait_ge(s_lo, n + 1)
                if h == 0:
                    since(pe, out_ready, t)
                last = split(Y[:], lambda a, c: sT[a][:, h, c, :],
                             lambda m, c: W["o"][m][:, (h * NH + c) * D:(h * NH + c + 1) * D], NH,
                             start=(h == 0), stop=(h == 1))
                if h:
                    last.then_inc(y_filled, 1)

            front(0, 0)
            pe.wait_ge(w_ready, 4)
            logits(0, 0)
            up(0, 0, 0)
            up(0, 0, 1)

            def step(t, r, more):
                s_transposes(t * 2, 0)
                if more:
                    front(t + 1, 1 - r)
                down(t * 2, t, 0)
                if more:
                    logits(t + 1, 1 - r)
                    up(t + 1, 1 - r, 0)
                s_transposes(t * 2 + 1, 1)
                down(t * 2 + 1, t, 1)
                if more:
                    up(t + 1, 1 - r, 1)

            for r in range(2):
                step(r, r, True)
            with pe.Fori(1, TILES // 2 - 1) as i:
                for r in range(2):
                    step(i * 2 + r, r, True)
            step(TILES - 2, 0, True)
            step(TILES - 1, 1, False)


def program(nc, x, ctx_1024, g_xattn, g_ffn, wq, wk, wv, wo, bo, gate_w, wu, wvf, wof, out):
    x2_dram = nc.dram_tensor("x2_scratch", tuple(x.shape), F32, kind="Internal").ap()
    with nc.sbuf_tensor("identity", [P, P], F32) as ident, nc.semaphore("identity_ready") as ident_ready:
        with nc.Block() as block:
            @block.gpsimd
            def _(pool):
                nc.gpsimd.memset(ident[:], 1.0).then_inc(ident_ready, 1)
                pool.wait_ge(ident_ready, 1)
                nc.gpsimd.affine_select(out=ident[:], in_=ident[:], compare_op=ALU.is_equal, fill=0.0, base=0,
                                        pattern=[[-1, P]], channel_multiplier=1).then_inc(ident_ready, 1)
                pool.wait_ge(ident_ready, 2)
        attention_phase(nc, x, ctx_1024, g_xattn, wq, wk, wv, wo, bo, x2_dram, ident)
        ffn_phase(nc, x2_dram, g_ffn, gate_w, wu, wvf, wof, out, ident)


_INS = ["x", "ctx_1024", "g_xattn", "g_ffn", "L0_xattn_Wq", "L0_xattn_Wk", "L0_xattn_Wv", "L0_xattn_Wo",
        "L0_xattn_bo", "L0_ffn_gate_w", "L0_ffn_Wu", "L0_ffn_Wv", "L0_ffn_Wo"]


def kernel(**inputs):
    import numpy as _np
    import concourse.bacc as _bacc
    from concourse import mybir as _mybir
    from concourse.bass_utils import run_bass_kernel_spmd as _run

    nc = _bacc.Bacc("TRN2", target_bir_lowering=False, num_devices=1)
    arrays, args = {}, []
    for name in _INS:
        a = _np.ascontiguousarray(inputs[name])
        arrays[f"in_{name}_dram"] = a
        args.append(nc.dram_tensor(f"in_{name}_dram", a.shape, _mybir.dt.from_np(a.dtype), kind="ExternalInput").ap())
    out = nc.dram_tensor("out_0_dram", (8, 512, 512), _mybir.dt.float32, kind="ExternalOutput").ap()
    program(nc, *args, out)
    r = _run(nc, [arrays], core_ids=[0])
    return r.results[0]["out_0_dram"]
```

```python
import concourse.bass as bass
from concourse import mybir
from contextlib import ExitStack

F32 = mybir.dt.float32
F16 = mybir.dt.float16
I32 = mybir.dt.int32
U32 = mybir.dt.uint32
ALU = mybir.AluOpType
ACT = mybir.ActivationFunctionType
AXX = mybir.AxisListType.X

P = 128
XS = 16.0
WS = 256.0
EPS = 1e-5
LN_CHAIN = 6


class Count:

    def __init__(self, value=0):
        self.set(value, value)

    def set(self, value, parity):
        self.value, self.parity = value, parity

    def take(self, n=1):
        now, self.bank = self.value, self.parity % 2
        self.value, self.parity = now + n, self.parity + n
        return now


def since(eng, sem, count):
    if not isinstance(count, int) or count > 0:
        eng.wait_ge(sem, count)


LN_CONSTANTS = (0.25, -0.5, XS)


def layernorm_factors(pool, link, stats, work, cst, rs, nb, n):
    v, a, y, d, s, m2 = (work[:, k, :] for k in range(6))
    quarter, neg_half, scale = (cst[:, k, 0:rs.shape[1]] for k in range(3))
    col = lambda k: stats[:, :, k:k + 1].rearrange("p t o -> p (t o)")
    pool.tensor_tensor(d, col(1), col(4), ALU.subtract)
    pool.tensor_tensor(s, col(1), col(4), ALU.add)
    link(pool.tensor_tensor(m2, col(2), col(5), ALU.add))
    pool.tensor_tensor(a, d, d, ALU.mult)
    pool.tensor_scalar(m2, m2, 1.0 / n, EPS, ALU.mult, ALU.add)
    link(pool.tensor_scalar(s, s, -0.5, None, ALU.mult))
    link(pool.tensor_tensor(a, a, quarter, ALU.mult))
    link(pool.tensor_tensor(v, a, m2, ALU.add))
    link(pool.tensor_tensor(y, v, neg_half, ALU.pow))
    link(pool.tensor_tensor(rs, y, scale, ALU.mult))
    return pool.tensor_tensor(nb, s, rs, ALU.mult)


def attention_phase(nc, x, ctx_in, g1, wq, wk, wv, wo, bo, x2_dram, ident, ln_cst):
    B, S, D = x.shape
    HD = 64
    KC = D // P
    TT = S // P
    PAIRS = D // P
    HB = 2 * PAIRS
    SC2 = XS * XS
    SHIFT = 44.0
    QS = 1.0 / WS

    xt = x.rearrange("b (t p) d -> b t p d", p=P)
    ct = ctx_in.rearrange("b (t p) d -> b t p d", p=P)
    x2t_d = x2_dram.rearrange("b (t p) d -> b t p d", p=P)

    PRE_UNITS = 2 * TT + TT + 4
    BATCH_UNITS = 2 * 8 + 2 * 6
    MX_UNITS = 2 * TT + 1
    PRE_HI, BATCH_HI = 2 * TT + TT + 4, 24

    ctx = ExitStack()
    with ctx:
        sb = lambda name, shape, dt=F32: ctx.enter_context(nc.sbuf_tensor(name, shape, dt))
        ps = lambda name, shape, dt=F32: ctx.enter_context(nc.psum_tensor(name, shape, dt))
        sem = lambda name: ctx.enter_context(nc.semaphore(name))

        W = {n: (sb(f"w{n}_hi", [P, KC, D], F16), sb(f"w{n}_lo", [P, KC, D], F16)) for n in "qkvo"}
        x_in = sb("x_in", [P, TT, D])
        c_in = sb("c_in", [P, TT, D])
        xn = sb("xn", [P, 2, D])
        xT = [(sb(f"xT_hi{r}", [P, KC, S], F16), sb(f"xT_lo{r}", [P, KC, S], F16)) for r in range(2)]
        cT = [(sb(f"cT_hi{r}", [P, KC, S], F16), sb(f"cT_lo{r}", [P, KC, S], F16)) for r in range(2)]
        native = {n: (sb(f"{n}_hi", [P, S], F16), sb(f"{n}_lo", [P, S], F16)) for n in "qk"}
        K1, K2, Q1, Q2 = (sb(n, [P, 4, 2, S], F16) for n in ("K1", "K2", "Q1", "Q2"))
        V = sb("V", [P, 2, TT, HB, 2 * HD + 1], F16)
        P32 = sb("P32", [P, TT, S])
        Ph = sb("Ph", [P, 2, TT, S], F16)
        Pl = sb("Pl", [P, 2, TT, S], F16)
        O = [sb(f"O{r}", [P, TT, D]) for r in range(2)]
        oT = (sb("oT_hi", [P, KC, P], F16), sb("oT_lo", [P, KC, P], F16))
        xr = sb("xr", [P, 2, D])
        xb = sb("xb", [P, 2, D])
        x2t = sb("x2t", [P, 2, D])
        tgbo = sb("tgbo", [P, D])
        bo_b = sb("bo_b", [P, D])
        gate = sb("gate1", [P, 3])
        stats = sb("stats", [P, TT, 6])
        work = sb("work", [P, 6, TT])
        rs = sb("rs", [P, TT])
        nb = sb("nb", [P, TT])
        mx = sb("mx", [P, 2, TT])
        mneg = sb("mneg", [P, 2 * TT])
        mrow = sb("mrow", [2 * TT, P], F16)
        rec = sb("rec", [P, 2, TT])

        ST = ps("ST", [P, 2, S])
        MX = ps("MX", [P, 2, S])
        PV = ps("PV", [P, 2, 4, P])
        G = ps("G", [P, 2, S])
        stage = {"q": P32, "k": O[0], "v": O[1], "o": P32}

        w_ld = {n: sem(f"w{n}_loaded") for n in "qkvo"}
        w_hi = sem("weight_hi_done")
        w_ready = sem("weights_ready")
        const_ld = sem("constants_loaded")
        tanh_done = sem("gate_tanh_done")
        gate_ready = sem("gate_ready")
        tgbo_ready = sem("gated_bias_ready")
        init_done = sem("pads_written")
        mrow_ready = sem("max_rows_ready")
        x_ld = [sem(f"x_loaded{t}") for t in range(TT)]
        c_ld = [sem(f"ctx_loaded{t}") for t in range(TT)]
        xr_ld = [sem(f"xr_loaded{r}") for r in range(2)]
        ln_ready = sem("ln_factors_ready")
        xn_ready = sem("xn_ready")
        chain = sem("vector_chain")
        pool_chain = sem("pool_chain")
        stats_ready = sem("row_statistics_ready")
        filled = sem("general_bank_filled")
        hi_done = sem("hi_part_written")
        evacuated = sem("general_bank_evacuated")
        qk_dma = [sem(f"qk_arranged{s}") for s in range(4)]
        m_dma = [sem(f"max_rows_placed{s}") for s in range(4)]
        mx_filled = sem("max_scores_filled")
        mx_taken = sem("row_max_taken")
        mneg_ready = sem("negated_max_ready")
        st_filled = sem("scores_filled")
        p_ready = sem("probs_f32_ready")
        ph_ready = sem("probs_hi_ready")
        pl_vec = sem("probs_lo_first_half")
        pl_pool = sem("probs_lo_second_half")
        pv_done = sem("pv_done")
        o_ready = sem("head_output_ready")
        xb_ready = sem("residual_plus_bias_ready")
        x2_st = [sem(f"x2_stored{r}") for r in range(2)]

        QK_DMAS = 12

        def at_batch(unit, b):
            unit.set(b * BATCH_UNITS + (PRE_UNITS - 8), PRE_UNITS - 8)

        def slot_and_use(b, j):
            return j % 4, b + j // 4 + 1

        def batches(eng, unit, step):
            for j in range(4):
                step(0, j)
            with eng.Fori(0, (B - 4) // 2) as i:
                for r in (1, 2):
                    b = i * 2 + r
                    unit(b)
                    for j in range(4):
                        step(b, j, r % 2)
            for b in range(B - 3, B):
                unit(b)
                for j in range(4):
                    step(b, j, b % 2)

        block = ctx.enter_context(nc.Block())

        @block.sync
        def _(sp):
            for r in range(2):
                sp.sem_inc(x2_st[r], 16)

            def load_tile(b, t):
                sp.dma_start(x_in[:, t, :], xt[b, t]).then_inc(x_ld[t], 16)
                sp.dma_start(c_in[:, t, :], ct[b, t]).then_inc(c_ld[t], 16)

            def arrange(b, j, uq):
                s, use = slot_and_use(b, j)
                for n, (one, two) in (("q", (Q1, Q2)), ("k", (K1, K2))):
                    sp.wait_ge(evacuated, uq + 1 + (n == "k"))
                    hi, lo = native[n]
                    E, Od = slice(0, HD), slice(HD, P)
                    moves = [(one, E, 0, hi, E), (one, Od, 0, hi if n == "q" else lo, E),
                             (one, Od, 1, hi, Od), (one, E, 1, hi if n == "q" else lo, Od),
                             (two, E, 0, lo if n == "q" else hi, E), (two, Od, 1, lo if n == "q" else hi, Od)]
                    for dst, dp, h, src, sp_ in moves:
                        sp.dma_start(dst[dp, s, h, :], src[sp_, :]).then_inc(qk_dma[s], 16)

            def max_rows(b, j):
                s, use = slot_and_use(b, j)
                sp.wait_ge(mrow_ready, b * PAIRS + j + 1)
                for h, row in ((0, HD), (1, 0)):
                    sp.dma_start(Q2[row:row + 1, s, h, :].rearrange("p (a c) -> p a c", a=TT),
                                 mrow[TT * h:TT * h + TT, :]).then_inc(m_dma[s], 16)

            for t in range(TT):
                load_tile(0, t)
                if t == 0:
                    sp.dma_start(stage["q"][:], wq.rearrange("(c p) n -> p c n", p=P)).then_inc(w_ld["q"], 16)
                    sp.dma_start(stage["k"][:], wk.rearrange("(c p) n -> p c n", p=P)).then_inc(w_ld["k"], 16)
                    sp.dma_start(stage["v"][:], wv.rearrange("(c p) n -> p c n", p=P)).then_inc(w_ld["v"], 16)
            sp.dma_start(bo_b[:], bo.rearrange("(a n) -> a n", a=1).to_broadcast([P, D])).then_inc(const_ld, 16)
            sp.dma_start(gate[:, 0:1], g1.rearrange("(a n) -> a n", a=1).to_broadcast([P, 1])).then_inc(const_ld, 16)
            sp.wait_ge(w_ready, 1)
            sp.dma_start(stage["o"][:], wo.rearrange("(c p) n -> p c n", p=P)).then_inc(w_ld["o"], 16)
            u = 3 * TT
            sp.wait_ge(init_done, 4)
            arrange(0, 0, u)
            arrange(0, 1, u + 2)
            max_rows(0, 0)
            unit = Count(PRE_UNITS)

            def step(b, j, r=0):
                known = isinstance(b, int)
                more = not known or b < B - 1
                if j == 0 and known and b == 0:
                    for t in range(TT):
                        load_tile(1, t)
                uq = unit.take() if more or j < 2 else None
                uk = unit.take() if more or j < 2 else None
                w = not known or b > 0
                if w:
                    since(sp, x2_st[j % 2], (b * 2 - 1 + j // 2) * 16)
                    sp.dma_start(xr[:, j % 2, :], xt[b - 1, j]).then_inc(xr_ld[j % 2], 16)
                if uq is not None:
                    arrange(b, j + 2, uq)
                if w:
                    unit.take()
                if more:
                    unit.take(2 if j < 2 else 1)
                if more or j < 3:
                    max_rows(b, j + 1)
                if j == 2 and (not known or b < B - 2):
                    for t in range(TT):
                        load_tile(b + 2, t)
                if w:
                    sp.wait_ge(evacuated, unit.take() + 1)
                    sp.dma_start(x2t_d[b - 1, j], x2t[:, j % 2, :]).then_inc(x2_st[j % 2], 16)
                if more:
                    unit.take(2 if j < 2 else 1)

            batches(sp, lambda b: at_batch(unit, b), step)
            for j in range(4):
                sp.wait_ge(x2_st[j % 2], (B * 2 - 1 + j // 2) * 16)
                sp.dma_start(xr[:, j % 2, :], xt[B - 1, j]).then_inc(xr_ld[j % 2], 16)
                unit.take()
                sp.wait_ge(evacuated, unit.take() + 1)
                sp.dma_start(x2t_d[B - 1, j], x2t[:, j % 2, :]).then_inc(x2_st[j % 2], 16)
            for r in range(2):
                sp.wait_ge(x2_st[r], (B * 2 + 1) * 16)

        @block.gpsimd
        def _(pool):
            links = Count(0)

            def link(ins):
                ins.then_inc(pool_chain, 1)
                pool.wait_ge(pool_chain, links.take() + 1)

            def factors(b):
                pool.wait_ge(stats_ready, (b + 1) * TT)
                layernorm_factors(nc.gpsimd, link, stats, work, ln_cst, rs[:], nb[:], D).then_inc(ln_ready, 1)

            factors(0)
            pool.wait_ge(xn_ready, TT)
            factors(1)
            pool.wait_ge(tanh_done, 1)
            nc.gpsimd.tensor_scalar(tgbo[:], bo_b[:], gate[:, 1:2], None, ALU.mult).then_inc(tgbo_ready, 1)
            pool.wait_ge(tgbo_ready, 1)

            def step(b, j, r=0):
                known = isinstance(b, int)
                if not known or b > 0:
                    k = j % 2
                    pool.wait_ge(xr_ld[k], (b * 2 - 1 + j // 2) * 16)
                    since(pool, x2_st[k], (b * 2 - 1 + j // 2) * 16)
                    nc.gpsimd.tensor_tensor(xb[:, k, :], xr[:, k, :], tgbo[:], ALU.add).then_inc(xb_ready, 1)
                for hh in range(2):
                    hd = b * HB + 2 * j + hh
                    for c in (2, 3):
                        pool.wait_ge(ph_ready, hd * 4 + c + 1)
                        nc.gpsimd.tensor_tensor(Pl[:, hh, c, :], P32[:, c, :], Ph[:, hh, c, :],
                                                ALU.subtract).then_inc(pl_pool, 1)
                if j == 3 and (not known or b < B - 2):
                    factors(b + 2)

            batches(pool, lambda b: links.set(b * LN_CHAIN + 2 * LN_CHAIN, 0), step)
            for j in range(4):
                k = j % 2
                pool.wait_ge(xr_ld[k], (B * 2 - 1 + j // 2) * 16)
                pool.wait_ge(x2_st[k], (B * 2 - 1 + j // 2) * 16)
                nc.gpsimd.tensor_tensor(xb[:, k, :], xr[:, k, :], tgbo[:], ALU.add).then_inc(xb_ready, 1)

        @block.scalar
        def _(act):
            def hi_part(u, dst, scale):
                act.wait_ge(filled, u + 1)
                src = G[:, unit.bank, :]
                if dst.shape[-1] != S:
                    src = src.rearrange("p (c n) -> p c n", c=dst.shape[1])
                nc.scalar.activation(dst, src, ACT.Copy, scale=scale).then_inc(hi_done, 1)

            def normalise(n, t):
                act.wait_ge(ln_ready, n + 1)
                nc.scalar.activation(xn[:, t % 2, :], x_in[:, t, :], ACT.Identity,
                                     scale=rs[:, t:t + 1], bias=nb[:, t:t + 1]).then_inc(xn_ready, 1)

            def v_view(r, t, lo):
                return V[:, r, t, :, (HD + 1 if lo else 0):(2 * HD + 1 if lo else HD)]

            def exps(hd, hh, *chunks):
                for c in chunks:
                    act.wait_ge(st_filled, hd * 4 + c + 1)
                    since(act, pl_vec if c < 2 else pl_pool, hd * 2 + c % 2 - 1)
                    nc.scalar.activation(P32[:, c, :], ST[:, c % 2, :], ACT.Exp,
                                         scale=0.125 / SC2).then_inc(p_ready, 1)
                    since(act, pv_done, hd - 1)
                    nc.scalar.activation(Ph[:, hh, c, :], ST[:, c % 2, :], ACT.Exp,
                                         scale=0.125 / SC2).then_inc(ph_ready, 1)

            def weight_hi(n):
                act.wait_ge(w_ld[n], 16)
                nc.scalar.activation(W[n][0][:], stage[n][:], ACT.Copy, scale=WS).then_inc(w_hi, 1)

            weight_hi("q")
            weight_hi("k")
            unit = Count(0)

            def transposed(b, t, r):
                for dst, scale in ((xT[r][0], 1.0), (cT[r][0], XS)):
                    hi_part(unit.take(), dst[:, :, t * P:(t + 1) * P], scale)

            for t in range(TT):
                normalise(0, t)
                transposed(0, t, 0)
            weight_hi("v")
            weight_hi("o")
            act.wait_ge(const_ld, 32)
            nc.scalar.activation(gate[:, 1:2], gate[:, 0:1], ACT.Tanh).then_inc(tanh_done, 1)
            for t in range(TT):
                u = unit.take()
                act.wait_ge(filled, u + 1)
                nc.scalar.activation(v_view(0, t, False), G[:, unit.bank, :].rearrange("p (h d) -> p h d", d=HD),
                                     ACT.Copy, scale=QS).then_inc(hi_done, 1)
            for pair in range(2):
                for n in "qk":
                    if pair:
                        act.wait_ge(qk_dma[0], QK_DMAS * 16)
                    hi_part(unit.take(), native[n][0][:], QS)

            def step(b, j, r=0):
                known = isinstance(b, int)
                more = not known or b < B - 1
                w = not known or b > 0
                nr = 1 - r
                hd = b * HB + 2 * j

                def project_hi(n):
                    if more or j < 2:
                        s, use = slot_and_use(b, j + 1)
                        act.wait_ge(qk_dma[s], use * QK_DMAS * 16)
                        hi_part(unit.take(), native[n][0][:], QS)

                def side(t):
                    if j < 2:
                        transposed(b, t, nr)
                    else:
                        u = unit.take()
                        act.wait_ge(filled, u + 1)
                        nc.scalar.activation(v_view(nr, t, False), G[:, unit.bank, :].rearrange("p (h d) -> p h d", d=HD),
                                             ACT.Copy, scale=QS).then_inc(hi_done, 1)

                exps(hd, 0, 0, 1)
                project_hi("q")
                exps(hd, 0, 2, 3)
                if more and j < 2:
                    for t in (2 * j, 2 * j + 1):
                        normalise(b + 1, t)
                project_hi("k")
                exps(hd + 1, 1, 0)
                if w:
                    hi_part(unit.take(), oT[0][:], 1.0)
                exps(hd + 1, 1, 1)
                if more:
                    side(2 * (j % 2))
                exps(hd + 1, 1, 2)
                if w:
                    unit.take()
                exps(hd + 1, 1, 3)
                if more:
                    side(2 * (j % 2) + 1)

            batches(act, lambda b: at_batch(unit, b), step)
            for j in range(4):
                hi_part(unit.take(), oT[0][:], 1.0)
                unit.take()

        @block.vector
        def _(dve):
            links = Count(0)

            def link(ins):
                ins.then_inc(chain, 1)
                dve.wait_ge(chain, links.take() + 1)

            unit = Count(0)
            hi = Count(0)

            def lo_part(dst, hi_view, scale):
                u = unit.take()
                dve.wait_ge(hi_done, hi.take() + 1)
                src = G[:, unit.bank, :]
                if dst.shape[-1] != S:
                    src = src.rearrange("p (c n) -> p c n", c=dst.shape[1])
                nc.vector.scalar_tensor_tensor(out=dst, in0=src, scalar=scale, in1=hi_view,
                                               op0=ALU.mult, op1=ALU.subtract).then_inc(evacuated, 1)

            def statistics(t, use):
                dve.wait_ge(x_ld[t], use * 16)
                nc.vector.bn_stats(stats[:, t, :], x_in[:, t, :]).then_inc(stats_ready, 1)

            def row_max(n, k, odd):
                dve.wait_ge(mx_filled, n + 1)
                nc.vector.tensor_reduce(out=mx[:, k // TT, k % TT:k % TT + 1], in_=MX[:, (k + odd) % 2, :], axis=AXX,
                                        op=ALU.max).then_inc(mx_taken, 1)

            def negate(n):
                dve.wait_ge(mx_taken, n)
                nc.vector.tensor_scalar(mneg[:], mx[:].rearrange("p h t -> p (h t)"), -1.0 / SC2, SHIFT,
                                        ALU.mult, ALU.add).then_inc(mneg_ready, 1)

            def max_rows(n, odd):
                dve.wait_ge(mx_filled, n + 1)
                nc.vector.tensor_copy(mrow[:], MX[0:2 * TT, odd, 0:P]).then_inc(mrow_ready, 1)

            def transposed(t, r):
                for (hi_t, lo_t), scale in ((xT[r], 1.0), (cT[r], XS)):
                    c = slice(t * P, (t + 1) * P)
                    lo_part(lo_t[:, :, c], hi_t[:, :, c], scale)

            def v_lo(t, r):
                u = unit.take()
                dve.wait_ge(hi_done, hi.take() + 1)
                nc.vector.scalar_tensor_tensor(
                    out=V[:, r, t, :, HD + 1:], in0=G[:, unit.bank, :].rearrange("p (h d) -> p h d", d=HD), scalar=QS,
                    in1=V[:, r, t, :, 0:HD], op0=ALU.mult, op1=ALU.subtract).then_inc(evacuated, 1)

            def head_out(hd, j, hh, r):
                dve.wait_ge(pv_done, hd + 1)
                link(nc.vector.reciprocal(rec[:, hh, :], PV[:, hh, :, HD:HD + 1].rearrange("p t o -> p (t o)")))
                h = 2 * j + hh
                nc.vector.tensor_tensor(O[r][:, :, h * HD:(h + 1) * HD], PV[:, hh, :, 0:HD],
                                        rec[:, hh, :].unsqueeze(2).to_broadcast([P, TT, HD]),
                                        ALU.mult).then_inc(o_ready, 1)

            def probs_lo(hd, hh, c):
                dve.wait_ge(ph_ready, hd * 4 + c + 1)
                nc.vector.tensor_tensor(Pl[:, hh, c, :], P32[:, c, :], Ph[:, hh, c, :],
                                        ALU.subtract).then_inc(pl_vec, 1)

            def x2_rows(w, j, uses):
                u = unit.take()
                dve.wait_ge(filled, u + 1)
                dve.wait_ge(xb_ready, w + 1)
                since(dve, x2_st[j % 2], uses)
                nc.vector.scalar_tensor_tensor(out=x2t[:, j % 2, :], in0=G[:, unit.bank, :], scalar=gate[:, 2:3],
                                               in1=xb[:, j % 2, :], op0=ALU.mult, op1=ALU.add).then_inc(evacuated, 1)

            def weight_lo(n, k):
                dve.wait_ge(w_hi, k + 1)
                nc.vector.scalar_tensor_tensor(out=W[n][1][:].rearrange("p c n -> p (c n)"),
                                               in0=stage[n][:].rearrange("p c n -> p (c n)"), scalar=WS,
                                               in1=W[n][0][:].rearrange("p c n -> p (c n)"),
                                               op0=ALU.mult, op1=ALU.subtract).then_inc(w_ready, 1)

            for t in range(TT):
                statistics(t, 1)
            for h, dp in ((0, slice(HD, P)), (1, slice(0, HD))):
                nc.vector.memset(K2[dp, :, h, :], 0.0).then_inc(init_done, 1)
                nc.vector.memset(Q2[dp, :, h, :], 0.0).then_inc(init_done, 1)
            dve.wait_ge(init_done, 4)
            for h, row in ((0, HD), (1, 0)):
                nc.vector.memset(K2[row:row + 1, :, h, :], SC2).then_inc(init_done, 1)
            nc.vector.memset(V[:, :, :, :, HD:HD + 1], 1.0).then_inc(init_done, 1)
            weight_lo("q", 0)
            weight_lo("k", 1)
            for t in range(TT):
                transposed(t, 0)
            weight_lo("v", 2)
            weight_lo("o", 3)
            dve.wait_ge(tanh_done, 1)
            nc.vector.tensor_scalar(gate[:, 2:3], gate[:, 1:2], 1.0 / (XS * WS), None, ALU.mult).then_inc(gate_ready, 1)
            dve.wait_ge(gate_ready, 1)
            for t in range(TT):
                v_lo(t, 0)
            for pair in range(2):
                for n in "qk":
                    lo_part(native[n][1][:], native[n][0][:], QS)
            for k in range(8):
                row_max(k, k, 0)
            negate(8)
            max_rows(8, 0)
            for t in range(TT):
                statistics(t, 2)

            def step(b, j, r=0):
                known = isinstance(b, int)
                more = not known or b < B - 1
                w = not known or b > 0
                nr = 1 - r
                hd = b * HB + 2 * j
                mxn = (b * PAIRS + (j + 1)) * MX_UNITS
                odd = (j + 1) % 2
                nmax = more or j < 3

                def maxima(*ks):
                    for k in ks:
                        if nmax:
                            row_max(mxn + k, k, odd)

                def side(t):
                    transposed(t, nr) if j < 2 else v_lo(t, nr)

                def proj_lo(n):
                    if more or j < 2:
                        lo_part(native[n][1][:], native[n][0][:], QS)

                maxima(0, 1, 2, 3)
                probs_lo(hd, 0, 0)
                proj_lo("q")
                maxima(4, 5)
                probs_lo(hd, 0, 1)
                maxima(6, 7)
                if nmax:
                    negate((b * PAIRS + (j + 2)) * (2 * TT))
                proj_lo("k")
                if w or j:
                    head_out(hd - 1, (j - 1) % 4, 1, r if j else nr)
                if nmax:
                    max_rows(mxn + 8, odd)
                if w:
                    lo_part(oT[1][:], oT[0][:], 1.0)
                probs_lo(hd + 1, 1, 0)
                if more:
                    side(2 * (j % 2))
                if j == 3 and (not known or b < B - 2):
                    for t in range(TT):
                        statistics(t, b + 3)
                probs_lo(hd + 1, 1, 1)
                if w:
                    x2_rows(b * 4 - 4 + j, j, (b * 2 - 1 + j // 2) * 16)
                head_out(hd, j, 0, r)
                if more:
                    side(2 * (j % 2) + 1)

            def at_counts(b):
                at_batch(unit, b)
                hi.value = b * BATCH_HI + (PRE_HI - 4)
                links.value = b * HB + (-1)

            batches(dve, at_counts, step)
            head_out(B * HB - 1, 3, 1, (B - 1) % 2)
            for j in range(4):
                lo_part(oT[1][:], oT[0][:], 1.0)
                x2_rows(B * 4 - 4 + j, j, (B * 2 - 1 + j // 2) * 16)

        @block.tensor
        def _(pe):
            unit = Count(0)

            def bank():
                u = unit.take()
                since(pe, evacuated, u - 1)
                return u, G[:, unit.bank, :]

            def product(out, parts, n0=0, n1=None):
                n1 = len(parts) if n1 is None else n1
                for n in range(n0, n1):
                    a, m = parts[n]
                    last = nc.tensor.matmul(out, a, m, start=(n == 0), stop=(n == len(parts) - 1))
                return last

            def split_parts(stat, mov):
                return [(stat(a, c), mov(m, c)) for c in range(KC) for a, m in ((0, 0), (0, 1), (1, 0))]

            def transposes(src):
                u, g = bank()
                for c in range(KC):
                    last = nc.tensor.transpose(g[:, c * P:(c + 1) * P], src[:, c * P:(c + 1) * P], ident[:])
                last.then_inc(filled, 1)

            def x_tile(t, n):
                pe.wait_ge(xn_ready, n + 1)
                transposes(xn[:, t % 2, :])

            def c_tile(t, use):
                pe.wait_ge(c_ld[t], use * 16)
                transposes(c_in[:, t, :])

            def qk_parts(n, pair, r):
                act_t = xT[r] if n == "q" else cT[r]
                return split_parts(lambda a, c: W[n][a][:, c, pair * P:(pair + 1) * P],
                                   lambda m, c: act_t[m][:, c, :])

            def v_parts(t, r):
                return split_parts(lambda a, c: cT[r][a][:, c, t * P:(t + 1) * P], lambda m, c: W["v"][m][:, c, :])

            def row_max_scores(n, k, s, use, odd, pair):
                h, t = k // TT, k % TT
                if k == 0:
                    pe.wait_ge(qk_dma[s], use * QK_DMAS * 16)
                if k == 1:
                    since(pe, mrow_ready, pair)
                else:
                    since(pe, mx_taken, pair * (2 * TT) + k - (1 if k > 1 else 0))
                nc.tensor.matmul(MX[:, (k + odd) % 2, :], Q1[:, s, h, t * P:(t + 1) * P], K1[:, s, h, :],
                                 start=True, stop=True).then_inc(mx_filled, 1)

            def max_transpose(pair, odd):
                pe.wait_ge(mneg_ready, pair + 1)
                nc.tensor.transpose(MX[0:2 * TT, odd, 0:P], mneg[:], ident[:]).then_inc(mx_filled, 1)

            def scores(b, j, k):
                hh, c = divmod(k, TT)
                n = b * (HB * TT) + 8 * j + k
                if k == 0:
                    pe.wait_ge(m_dma[j], (b + 1) * 32)
                since(pe, ph_ready, n - 1)
                cols = slice(c * P, (c + 1) * P)
                nc.tensor.matmul(ST[:, c % 2, :], K1[:, j, hh, cols], Q1[:, j, hh, :], start=True, stop=False)
                nc.tensor.matmul(ST[:, c % 2, :], K2[:, j, hh, cols], Q2[:, j, hh, :],
                                 start=False, stop=True).then_inc(st_filled, 1)

            def weighted(hd, h, r, t):
                hh = h % 2
                if t == 0:
                    pe.wait_ge(pl_vec, hd * 2 + 2)
                    pe.wait_ge(pl_pool, hd * 2 + 2)
                    since(pe, o_ready, hd - 1)
                cols = slice(t * P, (t + 1) * P)
                out = PV[:, hh, t, :]
                for c in range(TT):
                    nc.tensor.matmul(out[:, 0:HD + 1], Ph[:, hh, c, cols], V[:, r, c, h, 0:HD + 1],
                                     start=(c == 0), stop=False)
                    nc.tensor.matmul(out[:, 0:HD], Ph[:, hh, c, cols], V[:, r, c, h, HD + 1:],
                                     start=False, stop=False)
                    last = nc.tensor.matmul(out[:, 0:HD + 1], Pl[:, hh, c, cols], V[:, r, c, h, 0:HD + 1],
                                            start=False, stop=(c == TT - 1))
                if t == TT - 1:
                    last.then_inc(pv_done, 1)

            def out_project(split):
                u, g = bank()
                pe.wait_ge(evacuated, split + 1)
                product(g, split_parts(lambda a, c: oT[a][:, c, :],
                                       lambda m, c: W["o"][m][:, c, :])).then_inc(filled, 1)

            for t in range(TT):
                x_tile(t, t)
                c_tile(t, 1)
            pe.wait_ge(w_ready, 3)
            pe.wait_ge(evacuated, 2 * TT)
            for t in range(TT):
                u, g = bank()
                product(g, v_parts(t, 0)).then_inc(filled, 1)
            for pair in range(2):
                for n in "qk":
                    u, g = bank()
                    product(g, qk_parts(n, pair, 0)).then_inc(filled, 1)
            for k in range(8):
                row_max_scores(k, k, 0, 1, 0, 0)
            max_transpose(0, 0)
            pe.wait_ge(init_done, 7)
            pe.wait_ge(w_ready, 4)

            def step(b, j, r=0):
                known = isinstance(b, int)
                more = not known or b < B - 1
                w = not known or b > 0
                nr = 1 - r
                hd = b * HB + 2 * j
                odd = (j + 1) % 2
                s, use = slot_and_use(b, j + 1)
                qk_r = r if j < 2 else nr

                def maxima(*ks):
                    for k in ks:
                        if more or j < 3:
                            row_max_scores(0, k, s, use, odd, b * PAIRS + (j + 1))

                proj = more or j < 2
                parts = {n: qk_parts(n, (j + 2) % 4, qk_r) for n in "qk"}

                def side(t):
                    if j < 2:
                        x_tile(t, b * 4 + 4 + t)
                        c_tile(t, b + 2)
                    else:
                        u, g = bank()
                        product(g, v_parts(t, nr)).then_inc(filled, 1)

                def last_head(*ts):
                    for t in ts:
                        if w or j:
                            weighted(hd - 1, (2 * j - 1) % HB, r if j else nr, t)

                for k in range(4):
                    n = "qk"[k // 2]
                    scores(b, j, k)
                    maxima(2 * k)
                    if proj and k % 2 == 0:
                        u, g = bank()
                        if j == 2 and k == 0:
                            pe.wait_ge(evacuated, u)
                        product(g, parts[n], 0, 6)
                    maxima(2 * k + 1)
                    if k % 2 == 0:
                        last_head(k // 2)
                    if proj and k % 2 == 1:
                        product(g, parts[n], 6).then_inc(filled, 1)
                scores(b, j, 4)
                last_head(2, 3)
                if w:
                    pe.wait_ge(o_ready, b * HB)
                    split = unit.value
                    transposes(O[nr][:, j, :])
                if more or j < 3:
                    max_transpose(b * PAIRS + j + 1, odd)
                scores(b, j, 5)
                if more:
                    side(2 * (j % 2))
                scores(b, j, 6)
                weighted(hd, 2 * j, r, 0)
                weighted(hd, 2 * j, r, 1)
                if w:
                    out_project(split)
                scores(b, j, 7)
                weighted(hd, 2 * j, r, 2)
                weighted(hd, 2 * j, r, 3)
                if more:
                    side(2 * (j % 2) + 1)

            batches(pe, lambda b: at_batch(unit, b), step)
            for t in range(TT):
                weighted(B * HB - 1, HB - 1, (B - 1) % 2, t)
            pe.wait_ge(o_ready, B * HB)
            for j in range(4):
                split = unit.value
                transposes(O[(B - 1) % 2][:, j, :])
                out_project(split)


def ffn_phase(nc, x2_dram, g2, gate_w, wu, wv, wo, out, ident, ln_cst):
    B, S, D = x2_dram.shape
    E, _, R = wu.shape
    KC = D // P
    TT = S // P
    FILLS = KC + 2
    CS = 256.0
    S_SCALE = XS * 0.5 / (XS * WS) ** 2 / CS
    x2_d = x2_dram.rearrange("b (t p) d -> b p t d", p=P)
    out_d = out.rearrange("b (t p) d -> b t p d", p=P)

    ctx = ExitStack()
    with ctx:
        sb = lambda name, shape, dt=F32: ctx.enter_context(nc.sbuf_tensor(name, shape, dt))
        ps = lambda name, shape, dt=F32: ctx.enter_context(nc.psum_tensor(name, shape, dt))
        sem = lambda name: ctx.enter_context(nc.semaphore(name))
        stage = {n: sb(f"f{n}_stage", [P, E, D]) for n in "uvo"}
        g_stage = sb("gate_w_stage", [P, KC, E])
        W = {n: (sb(f"f{n}_hi", [P, E, D], F16), sb(f"f{n}_lo", [P, E, D], F16)) for n in "uvo"}
        Wg = (sb("fg_hi", [P, KC, E], F16), sb("fg_lo", [P, KC, E], F16))
        x2s = sb("x2s", [P, 2, TT, D])
        xn = sb("xn2", [P, TT, D])
        xT = (sb("x2T_hi", [P, 2, KC, S], F16), sb("x2T_lo", [P, 2, KC, S], F16))
        th = sb("th", [P, S])
        a_sb = sb("a_sb", [P, S])
        aw = sb("aw", [P, S])
        s32 = sb("s32", [P, S])
        sT = (sb("sT_hi", [P, 2, S], F16), sb("sT_lo", [P, 2, S], F16))
        res = sb("res", [P, TT, D])
        stats = sb("stats2", [P, TT, 6])
        work = sb("work2", [P, 6, TT])
        rs = sb("rs2", [P, TT])
        nb = sb("nb2", [P, TT])
        lg = sb("lg", [P, TT, E])
        top = sb("top", [P, TT, 8])
        took = sb("took", [P, 1])
        idx = sb("idx", [P, TT, 8], U32)
        idf = sb("idf", [P, TT, 2])
        gap = sb("gap", [P, TT])
        gexp = sb("gexp", [P, TT])
        den = sb("den", [P, TT])
        w12 = sb("w12", [P, 2, TT])
        cw = sb("cw", [P, 2, TT, E])
        cw_h = sb("cw_h", [P, TT, E], F16)
        cw_hl = sb("cw_hl", [P, TT, 2 * E])
        wT = sb("wT", [2 * E, 2, S], F16)
        pick = sb("pick", [2 * E, E, P], F16)
        iota = sb("iota", [P, E])
        gate = sb("gate2", [P, 3])

        U = ps("U", [P, S])
        Vp = ps("Vp", [P, S])
        WB = ps("WB", [P, S])
        M = ps("M", [P, S])
        Y = ps("Y", [P, TT, D])

        g_ld = sem("gate_w_loaded")
        w_ld = [sem(f"expert{e}_loaded") for e in range(E)]
        const_ld = sem("f_constants_loaded")
        iota_done, pick_done = sem("iota_done"), sem("pick_done")
        tanh_done, gate_ready = sem("f_tanh_done"), sem("f_gate_ready")
        w_hi, w_ready = sem("f_weight_hi"), sem("f_weights_ready")
        x_ld = [sem(f"x2_loaded{r}") for r in range(2)]
        st = sem("out_stored")
        chain, pool_chain = sem("f_vector_chain"), sem("f_pool_chain")
        stats_ready, ln_ready, xn_ready = sem("f_stats_ready"), sem("f_ln_ready"), sem("f_xn_ready")
        m_filled, t_hi, m_free = sem("misc_bank_filled"), sem("x2T_hi_written"), sem("misc_bank_free")
        gap_ready, exp_ready, cw_ready = sem("logit_gap_ready"), sem("gap_exp_ready"), sem("expert_weights_ready")
        u_filled, v_filled = sem("u_filled"), sem("v_filled")
        tanh_ready, a_done, aw_done, s_done = (sem("tanh_ready"), sem("u_bank_free"), sem("weight_bank_free"),
                                               sem("v_bank_free"))
        s_hi, s_lo = sem("sT_hi_written"), sem("sT_lo_written")
        y_filled, out_ready = sem("y_tiles_done"), sem("out_ready")
        block = ctx.enter_context(nc.Block())

        def groups(eng, group):
            group(0, 0, 1, True, True)
            with eng.Fori(0, B // 2 - 1) as i:
                group(i * 2 + 1, 1, i + 2, False, True)
                group(i * 2 + 2, 0, i + 2, False, True)
            group(B - 1, 1, 0, False, False)

        @block.sync
        def _(sp):
            sp.dma_start(x2s[:, 0], x2_d[0]).then_inc(x_ld[0], 16)
            sp.dma_start(g_stage[:], gate_w.rearrange("(c p) e -> p c e", p=P)).then_inc(g_ld, 16)
            sp.dma_start(gate[:, 0:1], g2.rearrange("(a n) -> a n", a=1).to_broadcast([P, 1])).then_inc(const_ld, 16)
            for e in range(E):
                for n, w in (("u", wu), ("v", wv)):
                    sp.dma_start(stage[n][:, e, :].rearrange("p (c r) -> p c r", c=KC),
                                 w[e].rearrange("(c p) r -> p c r", p=P)).then_inc(w_ld[e], 16)
                sp.dma_start(stage["o"][:, e, :], wo[e]).then_inc(w_ld[e], 16)
                if e == 1:
                    sp.dma_start(x2s[:, 1], x2_d[1]).then_inc(x_ld[1], 16)

            def store(b):
                for t in range(TT):
                    sp.wait_ge(out_ready, b * TT + (t + 1))
                    sp.dma_start(out_d[b, t], res[:, t, :]).then_inc(st, 16)

            def group(b, r, use, first, more):
                if not first:
                    store(b - 1)
                    if more:
                        sp.dma_start(x2s[:, 1 - r], x2_d[b + 1]).then_inc(x_ld[1 - r], 16)

            groups(sp, group)
            store(B - 1)
            sp.wait_ge(st, B * TT * 16)

        @block.gpsimd
        def _(pool):
            links = Count(0)

            def link(ins):
                ins.then_inc(pool_chain, 1)
                pool.wait_ge(pool_chain, links.take() + 1)

            def front(f):
                links.set(f * LN_CHAIN, 0)
                pool.wait_ge(stats_ready, f + 1)
                layernorm_factors(nc.gpsimd, link, stats, work, ln_cst, rs[:], nb[:], D).then_inc(ln_ready, 1)

            nc.gpsimd.iota(iota[:], [[1, E]], base=0, channel_multiplier=0,
                           allow_small_or_imprecise_dtypes=True).then_inc(iota_done, 1)
            front(0)

            def group(b, r, use, first, more):
                if more:
                    front(b + 1)

            groups(pool, group)

        @block.scalar
        def _(act):
            def weight_hi(e):
                act.wait_ge(w_ld[e], 3 * 16)
                for n in "uvo":
                    nc.scalar.activation(W[n][0][:, e, :], stage[n][:, e, :], ACT.Copy, scale=WS).then_inc(w_hi, 1)

            def normalise(f, r):
                act.wait_ge(ln_ready, f + 1)
                for t in range(TT):
                    last = nc.scalar.activation(xn[:, t, :], x2s[:, r, t, :], ACT.Identity, scale=rs[:, t:t + 1],
                                                bias=nb[:, t:t + 1])
                last.then_inc(xn_ready, 1)

            def transposed_hi(f, r, c):
                act.wait_ge(m_filled, f * FILLS + (c + 1))
                nc.scalar.activation(xT[0][:, r, c, :], M[:], ACT.Copy).then_inc(t_hi, 1)

            def gap_exp(f):
                act.wait_ge(gap_ready, f + 1)
                nc.scalar.activation(gexp[:], gap[:], ACT.Exp).then_inc(exp_ready, 1)

            act.wait_ge(g_ld, 16)
            nc.scalar.activation(Wg[0][:], g_stage[:], ACT.Copy, scale=WS).then_inc(w_hi, 1)
            act.wait_ge(const_ld, 16)
            nc.scalar.activation(gate[:, 1:2], gate[:, 0:1], ACT.Tanh).then_inc(tanh_done, 1)
            normalise(0, 0)
            for c in range(KC):
                transposed_hi(0, 0, c)
            weight_hi(0)
            gap_exp(0)
            weight_hi(1)

            def group(b, r, use, first, more):
                for e in range(E):
                    n = b * E + e
                    act.wait_ge(u_filled, n + 1)
                    nc.scalar.activation(th[:], U[:], ACT.Tanh, scale=0.5 / (XS * WS)).then_inc(tanh_ready, 1)
                    if more and e in (3, 4):
                        transposed_hi(b + 1, 1 - r, (e - 3) * 2)
                    if more and e == 6:
                        gap_exp(b + 1)
                    act.wait_ge(s_done, n + 1)
                    since(act, y_filled, (n - 1) * TT)
                    nc.scalar.activation(sT[0][:, e % 2, :], s32[:], ACT.Copy).then_inc(s_hi, 1)
                    if more and e == 2:
                        normalise(b + 1, 1 - r)
                    if more and e in (3, 4):
                        transposed_hi(b + 1, 1 - r, (e - 3) * 2 + 1)
                    if first and e + 2 < E:
                        weight_hi(e + 2)

            groups(act, group)

        @block.vector
        def _(dve):
            links = Count(0)

            def link(ins):
                ins.then_inc(chain, 1)
                dve.wait_ge(chain, links.take() + 1)

            def low(src, hi, lo):
                return nc.vector.scalar_tensor_tensor(out=lo, in0=src, scalar=WS, in1=hi, op0=ALU.mult,
                                                      op1=ALU.subtract).then_inc(w_ready, 1)

            def weight_lo(e):
                for k, n in enumerate("uvo"):
                    dve.wait_ge(w_hi, 1 + 3 * e + (k + 1))
                    low(stage[n][:, e, :], W[n][0][:, e, :], W[n][1][:, e, :])

            def statistics(r, use):
                dve.wait_ge(x_ld[r], use * 16)
                for t in range(TT):
                    last = nc.vector.bn_stats(stats[:, t, :], x2s[:, r, t, :])
                last.then_inc(stats_ready, 1)

            def transposed_lo(f, r, c):
                dve.wait_ge(t_hi, f * KC + (c + 1))
                nc.vector.tensor_tensor(xT[1][:, r, c, :], M[:], xT[0][:, r, c, :], ALU.subtract).then_inc(m_free, 1)

            def best_two(f):
                dve.wait_ge(m_filled, f * FILLS + (KC + 1))
                nc.vector.tensor_scalar(lg[:].rearrange("p t e -> p (t e)"), M[:, 0:TT * E], 1.0 / (XS * WS), None,
                                        ALU.mult).then_inc(m_free, 1)
                dve.wait_ge(m_free, f * FILLS + (KC + 1))
                nc.vector.tensor_copy(took[:], lg[:, 0, 0:1])
                for t in range(TT):
                    last = nc.vector.max(top[:, t, :], lg[:, t, :])
                link(last)
                nc.vector.tensor_tensor(gap[:], top[:, :, 1:2].rearrange("p t o -> p (t o)"),
                                        top[:, :, 0:1].rearrange("p t o -> p (t o)"), ALU.subtract).then_inc(gap_ready, 1)
                for t in range(TT):
                    last = nc.vector.max_index(idx[:, t, :], top[:, t, :], lg[:, t, :])
                link(last)
                link(nc.vector.tensor_copy(idf[:], idx[:, :, 0:2]))

            def expert_weights(f):
                dve.wait_ge(exp_ready, f + 1)
                link(nc.vector.tensor_scalar(den[:], gexp[:], 1.0, 1.0 / CS, ALU.add, ALU.mult))
                link(nc.vector.reciprocal(w12[:, 0, :], den[:]))
                link(nc.vector.tensor_tensor(w12[:, 1, :], gexp[:], w12[:, 0, :], ALU.mult))
                for t in range(TT):
                    for k in range(2):
                        last = nc.vector.tensor_scalar(cw[:, k, t, :], iota[:], idf[:, t, k:k + 1], w12[:, k, t:t + 1],
                                                       ALU.is_equal, ALU.mult)
                link(last)
                link(nc.vector.tensor_tensor(cw[:, 0], cw[:, 0], cw[:, 1], ALU.add))
                link(nc.vector.tensor_copy(cw_h[:], cw[:, 0]))
                nc.vector.tensor_copy(cw_hl[:, :, 0:E], cw_h[:])
                nc.vector.tensor_tensor(cw_hl[:, :, E:2 * E], cw[:, 0], cw_h[:], ALU.subtract).then_inc(cw_ready, 1)

            def weights_in_rows(f, r):
                dve.wait_ge(m_filled, f * FILLS + FILLS)
                nc.vector.tensor_copy(wT[:, r, :], M[0:2 * E, :]).then_inc(m_free, 1)

            def evacuate(b, r):
                since(dve, st, b * (TT * 16))
                for t in range(TT):
                    dve.wait_ge(y_filled, (b * E + (E - 1)) * TT + (t + 1))
                    nc.vector.scalar_tensor_tensor(out=res[:, t, :], in0=Y[:, t, :], scalar=gate[:, 2:3],
                                                   in1=x2s[:, r, t, :], op0=ALU.mult, op1=ALU.add).then_inc(out_ready, 1)

            statistics(0, 1)
            dve.wait_ge(w_hi, 1)
            low(g_stage[:], Wg[0][:], Wg[1][:])
            spread = lambda k: ident[0:2 * E, k * E:(k + 1) * E].unsqueeze(2).to_broadcast([2 * E, E, P])
            nc.vector.tensor_tensor(pick[:], spread(0), spread(1), ALU.add).then_inc(pick_done, 1)
            for c in range(KC):
                transposed_lo(0, 0, c)
            weight_lo(0)
            dve.wait_ge(iota_done, 1)
            best_two(0)
            expert_weights(0)
            weights_in_rows(0, 0)
            FRONT_LINKS = links.value
            dve.wait_ge(tanh_done, 1)
            nc.vector.tensor_scalar(gate[:, 2:3], gate[:, 1:2], 1.0 / (XS * WS), None, ALU.mult).then_inc(gate_ready, 1)
            dve.wait_ge(gate_ready, 1)
            weight_lo(1)

            def group(b, r, use, first, more):
                links.set(b * FRONT_LINKS + FRONT_LINKS, 0)
                for e in range(E):
                    n = b * E + e
                    dve.wait_ge(tanh_ready, n + 1)
                    nc.vector.scalar_tensor_tensor(out=a_sb[:], in0=th[:], scalar=1.0, in1=U[:], op0=ALU.add,
                                                   op1=ALU.mult).then_inc(a_done, 1)
                    dve.wait_ge(a_done, n + 1)
                    nc.vector.tensor_tensor(aw[:], a_sb[:], WB[:], ALU.mult).then_inc(aw_done, 1)
                    if more and e in (3, 4):
                        transposed_lo(b + 1, 1 - r, (e - 3) * 2)
                    if more and e == 7:
                        weights_in_rows(b + 1, 1 - r)
                    dve.wait_ge(aw_done, n + 1)
                    dve.wait_ge(v_filled, n + 1)
                    nc.vector.scalar_tensor_tensor(out=s32[:], in0=aw[:], scalar=S_SCALE, in1=Vp[:], op0=ALU.mult,
                                                   op1=ALU.mult).then_inc(s_done, 1)
                    dve.wait_ge(s_hi, n + 1)
                    nc.vector.tensor_tensor(sT[1][:, e % 2, :], s32[:], sT[0][:, e % 2, :], ALU.subtract).then_inc(s_lo, 1)
                    if e == 0 and not first:
                        evacuate(b - 1, 1 - r)
                    if more and e == 1:
                        statistics(1 - r, use)
                    if more and e in (3, 4):
                        transposed_lo(b + 1, 1 - r, (e - 3) * 2 + 1)
                    if more and e == 5:
                        best_two(b + 1)
                    if more and e == 6:
                        expert_weights(b + 1)
                    if first and e + 2 < E:
                        weight_lo(e + 2)

            groups(dve, group)
            evacuate(B - 1, (B - 1) % 2)

        @block.tensor
        def _(pe):
            PASSES = ((0, 0), (0, 1), (1, 0))

            def transposes(f, c):
                since(pe, m_free, f * FILLS + c)
                for t in range(TT):
                    last = nc.tensor.transpose(M[:, t * P:(t + 1) * P], xn[:, t, c * P:(c + 1) * P], ident[:])
                last.then_inc(m_filled, 1)

            def logits(f, r):
                pe.wait_ge(m_free, f * FILLS + KC)
                parts = [(a, m, c) for c in range(KC) for a, m in PASSES + ((1, 1),)]
                for t in range(TT):
                    for k, (a, m, c) in enumerate(parts):
                        last = nc.tensor.matmul(M[:, t * E:(t + 1) * E], xT[a][:, r, c, t * P:(t + 1) * P],
                                                Wg[m][:, c, :], start=k == 0, stop=k == len(parts) - 1)
                last.then_inc(m_filled, 1)

            def weight_rows(f):
                pe.wait_ge(cw_ready, f + 1)
                for t in range(TT):
                    last = nc.tensor.transpose(M[0:2 * E, t * P:(t + 1) * P], cw_hl[:, t, :], ident[:])
                last.then_inc(m_filled, 1)

            def up(n, dst, e, r, done):
                parts = [(m, a, c) for c in range(KC) for m, a in PASSES]
                for k, (m, a, c) in enumerate(parts):
                    last = nc.tensor.matmul(dst[:], W[n][m][:, e, c * P:(c + 1) * P], xT[a][:, r, c, :],
                                            start=k == 0, stop=k == len(parts) - 1)
                last.then_inc(done, 1)

            def down(b, n, e):
                pe.wait_ge(s_lo, n + 1)
                for t in range(TT):
                    if e == 0:
                        since(pe, out_ready, (b - 1) * TT + (t + 1))
                    for a, m in PASSES:
                        last = nc.tensor.matmul(Y[:, t, :], sT[a][:, e % 2, t * P:(t + 1) * P], W["o"][m][:, e, :],
                                                start=e == 0 and (a, m) == PASSES[0],
                                                stop=e == E - 1 and (a, m) == PASSES[-1])
                    last.then_inc(y_filled, 1)

            pe.wait_ge(xn_ready, 1)
            for c in range(KC):
                transposes(0, c)
            pe.wait_ge(w_ready, 1)
            logits(0, 0)
            pe.wait_ge(pick_done, 1)
            weight_rows(0)

            def group(b, r, use, first, more):
                for e in range(E):
                    n = b * E + e
                    if first:
                        pe.wait_ge(w_ready, 1 + 3 * (e + 1))
                    if e == 0:
                        pe.wait_ge(m_free, b * FILLS + FILLS)
                    since(pe, aw_done, n)
                    nc.tensor.matmul(WB[:], pick[:, e, :], wT[:, r, :], start=True, stop=True)
                    up("u", U, e, r, u_filled)
                    if more and e == 3:
                        pe.wait_ge(xn_ready, b + 2)
                    if more and e in (3, 4):
                        transposes(b + 1, (e - 3) * 2)
                    if more and e == 7:
                        weight_rows(b + 1)
                    since(pe, s_done, n)
                    up("v", Vp, e, r, v_filled)
                    if more and e == 5:
                        logits(b + 1, 1 - r)
                    if e > 0:
                        down(b, n - 1, e - 1)
                    elif not first:
                        down(b - 1, n - 1, E - 1)
                    if more and e in (3, 4):
                        transposes(b + 1, (e - 3) * 2 + 1)

            groups(pe, group)
            down(B - 1, B * E - 1, E - 1)


def program(nc, x, ctx_1024, g_xattn, g_ffn, wq, wk, wv, wo, bo, gate_w, wu, wvf, wof, out):
    x2_dram = nc.dram_tensor("x2_scratch", tuple(x.shape), F32, kind="Internal").ap()
    with nc.sbuf_tensor("identity", [P, P], F32) as ident, nc.semaphore("identity_ready") as ident_ready, \
            nc.sbuf_tensor("ln_constants", [P, len(LN_CONSTANTS), 4], F32) as ln_cst:
        with nc.Block() as block:
            @block.vector
            def _(dve):
                for k, value in enumerate(LN_CONSTANTS):
                    nc.vector.memset(ln_cst[:, k, :], value)

            @block.gpsimd
            def _(pool):
                nc.gpsimd.memset(ident[:], 1.0).then_inc(ident_ready, 1)
                pool.wait_ge(ident_ready, 1)
                nc.gpsimd.affine_select(out=ident[:], in_=ident[:], compare_op=ALU.is_equal, fill=0.0, base=0,
                                        pattern=[[-1, P]], channel_multiplier=1).then_inc(ident_ready, 1)
                pool.wait_ge(ident_ready, 2)
        attention_phase(nc, x, ctx_1024, g_xattn, wq, wk, wv, wo, bo, x2_dram, ident, ln_cst)
        ffn_phase(nc, x2_dram, g_ffn, gate_w, wu, wvf, wof, out, ident, ln_cst)


_INS = ["x", "ctx_1024", "g_xattn", "g_ffn", "L0_xattn_Wq", "L0_xattn_Wk", "L0_xattn_Wv", "L0_xattn_Wo",
        "L0_xattn_bo", "L0_ffn_gate_w", "L0_ffn_Wu", "L0_ffn_Wv", "L0_ffn_Wo"]


def kernel(**inputs):
    import numpy as _np
    import concourse.bacc as _bacc
    from concourse import mybir as _mybir
    from concourse.bass_utils import run_bass_kernel_spmd as _run

    nc = _bacc.Bacc("TRN2", target_bir_lowering=False, num_devices=1)
    arrays, args = {}, []
    for name in _INS:
        a = _np.ascontiguousarray(inputs[name])
        arrays[f"in_{name}_dram"] = a
        args.append(nc.dram_tensor(f"in_{name}_dram", a.shape, _mybir.dt.from_np(a.dtype), kind="ExternalInput").ap())
    out = nc.dram_tensor("out_0_dram", (8, 512, 512), _mybir.dt.float32, kind="ExternalOutput").ap()
    program(nc, *args, out)
    r = _run(nc, [arrays], core_ids=[0])
    return r.results[0]["out_0_dram"]
```

```python
import concourse.bass as bass
from concourse import mybir
from contextlib import ExitStack

F32 = mybir.dt.float32
F16 = mybir.dt.float16
U32 = mybir.dt.uint32
ALU = mybir.AluOpType
ACT = mybir.ActivationFunctionType
AXX = mybir.AxisListType.X

P = 128
XS = 16.0
WS = 256.0
EPS = 1e-5
LN_CHAIN = 6


class Count:

    def __init__(self, value=0):
        self.set(value, value)

    def set(self, value, parity):
        self.value, self.parity = value, parity

    def take(self, n=1):
        now, self.bank = self.value, self.parity % 2
        self.value, self.parity = now + n, self.parity + n
        return now


def since(eng, sem, count):
    if not isinstance(count, int) or count > 0:
        eng.wait_ge(sem, count)


LN_CONSTANTS = (0.25, -0.5, XS)


def layernorm_factors(pool, link, stats, work, cst, rs, nb, n):
    v, a, y, d, s, m2 = (work[:, k, :] for k in range(6))
    quarter, neg_half, scale = (cst[:, k, 0:rs.shape[1]] for k in range(3))
    col = lambda k: stats[:, :, k:k + 1].rearrange("p t o -> p (t o)")
    pool.tensor_tensor(d, col(1), col(4), ALU.subtract)
    pool.tensor_tensor(s, col(1), col(4), ALU.add)
    link(pool.tensor_tensor(m2, col(2), col(5), ALU.add))
    pool.tensor_tensor(a, d, d, ALU.mult)
    pool.tensor_scalar(m2, m2, 1.0 / n, EPS, ALU.mult, ALU.add)
    link(pool.tensor_scalar(s, s, -0.5, None, ALU.mult))
    link(pool.tensor_tensor(a, a, quarter, ALU.mult))
    link(pool.tensor_tensor(v, a, m2, ALU.add))
    link(pool.tensor_tensor(y, v, neg_half, ALU.pow))
    link(pool.tensor_tensor(rs, y, scale, ALU.mult))
    return pool.tensor_tensor(nb, s, rs, ALU.mult)


def attention_phase(nc, x, ctx_in, g1, wq, wk, wv, wo, bo, x2_dram, x2_stats, ident, ln_cst):
    B, S, D = x.shape
    HD = 64
    KC = D // P
    TT = S // P
    PAIRS = D // P
    HB = 2 * PAIRS
    SC2 = XS * XS
    SHIFT = 44.0
    QS = 1.0 / WS

    xt = x.rearrange("b (t p) d -> b t p d", p=P)
    ct = ctx_in.rearrange("b (t p) d -> b t p d", p=P)
    x2t_d = x2_dram.rearrange("b (t p) d -> b t p d", p=P)

    PRE_UNITS = 2 * TT + TT + 4
    BATCH_UNITS = 2 * 8 + 2 * 6
    MX_UNITS = 2 * TT + 1
    PRE_HI, BATCH_HI = 2 * TT + TT + 4, 24

    ctx = ExitStack()
    with ctx:
        sb = lambda name, shape, dt=F32: ctx.enter_context(nc.sbuf_tensor(name, shape, dt))
        ps = lambda name, shape, dt=F32: ctx.enter_context(nc.psum_tensor(name, shape, dt))
        sem = lambda name: ctx.enter_context(nc.semaphore(name))

        W = {n: (sb(f"w{n}_hi", [P, KC, D], F16), sb(f"w{n}_lo", [P, KC, D], F16)) for n in "qkvo"}
        x_in = sb("x_in", [P, TT, D])
        c_in = sb("c_in", [P, TT, D])
        xn = sb("xn", [P, 2, D])
        xT = [(sb(f"xT_hi{r}", [P, KC, S], F16), sb(f"xT_lo{r}", [P, KC, S], F16)) for r in range(2)]
        cT = [(sb(f"cT_hi{r}", [P, KC, S], F16), sb(f"cT_lo{r}", [P, KC, S], F16)) for r in range(2)]
        native = {n: (sb(f"{n}_hi", [P, S], F16), sb(f"{n}_lo", [P, S], F16)) for n in "qk"}
        K1, K2, Q1, Q2 = (sb(n, [P, 4, 2, S], F16) for n in ("K1", "K2", "Q1", "Q2"))
        V = sb("V", [P, 2, TT, HB, 2 * HD + 1], F16)
        P32 = sb("P32", [P, TT, S])
        Ph = sb("Ph", [P, 2, TT, S], F16)
        Pl = sb("Pl", [P, 2, TT, S], F16)
        O = [sb(f"O{r}", [P, TT, D]) for r in range(2)]
        oT = (sb("oT_hi", [P, KC, P], F16), sb("oT_lo", [P, KC, P], F16))
        xr = sb("xr", [P, 2, D])
        xb = sb("xb", [P, 2, D])
        x2t = sb("x2t", [P, 2, D])
        tgbo = sb("tgbo", [P, D])
        bo_b = sb("bo_b", [P, D])
        gate = sb("gate1", [P, 3])
        stats = sb("stats", [P, TT, 6])
        work = sb("work", [P, 6, TT])
        rs = sb("rs", [P, TT])
        nb = sb("nb", [P, TT])
        mx = sb("mx", [P, 2, TT])
        row_stats = sb("row_stats", [P, 6])
        mneg = sb("mneg", [P, 2 * TT])
        mrow = sb("mrow", [2 * TT, P], F16)
        rec = sb("rec", [P, 2, TT])

        ST = ps("ST", [P, 2, S])
        MX = ps("MX", [P, 2, S])
        PV = ps("PV", [P, 2, 4, P])
        G = ps("G", [P, 2, S])
        stage = {"q": P32, "k": O[0], "v": O[1], "o": P32}

        w_ld = {n: sem(f"w{n}_loaded") for n in "qkvo"}
        w_hi = sem("weight_hi_done")
        row_stats_ready = sem("x2_row_statistics")
        w_ready = sem("weights_ready")
        const_ld = sem("constants_loaded")
        tanh_done = sem("gate_tanh_done")
        gate_ready = sem("gate_ready")
        tgbo_ready = sem("gated_bias_ready")
        init_done = sem("pads_written")
        mrow_ready = sem("max_rows_ready")
        x_ld = [sem(f"x_loaded{t}") for t in range(TT)]
        c_ld = [sem(f"ctx_loaded{t}") for t in range(TT)]
        xr_ld = [sem(f"xr_loaded{r}") for r in range(2)]
        ln_ready = sem("ln_factors_ready")
        xn_ready = sem("xn_ready")
        chain = sem("vector_chain")
        pool_chain = sem("pool_chain")
        stats_ready = sem("row_statistics_ready")
        filled = sem("general_bank_filled")
        hi_done = sem("hi_part_written")
        evacuated = sem("general_bank_evacuated")
        qk_dma = [sem(f"qk_arranged{s}") for s in range(4)]
        m_dma = [sem(f"max_rows_placed{s}") for s in range(4)]
        mx_filled = sem("max_scores_filled")
        mx_taken = sem("row_max_taken")
        mneg_ready = sem("negated_max_ready")
        st_filled = sem("scores_filled")
        p_ready = sem("probs_f32_ready")
        ph_ready = sem("probs_hi_ready")
        pl_vec = sem("probs_lo_first_half")
        pl_pool = sem("probs_lo_second_half")
        pv_done = sem("pv_done")
        o_ready = sem("head_output_ready")
        xb_ready = sem("residual_plus_bias_ready")
        x2_st = [sem(f"x2_stored{r}") for r in range(2)]

        QK_DMAS = 12

        def at_batch(unit, b):
            unit.set(b * BATCH_UNITS + (PRE_UNITS - 8), PRE_UNITS - 8)

        def slot_and_use(b, j):
            return j % 4, b + j // 4 + 1

        def batches(eng, unit, step):
            for j in range(4):
                step(0, j)
            with eng.Fori(0, (B - 4) // 2) as i:
                for r in (1, 2):
                    b = i * 2 + r
                    unit(b)
                    for j in range(4):
                        step(b, j, r % 2)
            for b in range(B - 3, B):
                unit(b)
                for j in range(4):
                    step(b, j, b % 2)

        block = ctx.enter_context(nc.Block())

        @block.sync
        def _(sp):
            for r in range(2):
                sp.sem_inc(x2_st[r], 16)

            def load_tile(b, t):
                sp.dma_start(x_in[:, t, :], xt[b, t]).then_inc(x_ld[t], 16)
                sp.dma_start(c_in[:, t, :], ct[b, t]).then_inc(c_ld[t], 16)

            def arrange(b, j, uq):
                s, use = slot_and_use(b, j)
                for n, (one, two) in (("q", (Q1, Q2)), ("k", (K1, K2))):
                    sp.wait_ge(evacuated, uq + 1 + (n == "k"))
                    hi, lo = native[n]
                    E, Od = slice(0, HD), slice(HD, P)
                    moves = [(one, E, 0, hi, E), (one, Od, 0, hi if n == "q" else lo, E),
                             (one, Od, 1, hi, Od), (one, E, 1, hi if n == "q" else lo, Od),
                             (two, E, 0, lo if n == "q" else hi, E), (two, Od, 1, lo if n == "q" else hi, Od)]
                    for dst, dp, h, src, sp_ in moves:
                        sp.dma_start(dst[dp, s, h, :], src[sp_, :]).then_inc(qk_dma[s], 16)

            def max_rows(b, j):
                s, use = slot_and_use(b, j)
                sp.wait_ge(mrow_ready, b * PAIRS + j + 1)
                for h, row in ((0, HD), (1, 0)):
                    sp.dma_start(Q2[row:row + 1, s, h, :].rearrange("p (a c) -> p a c", a=TT),
                                 mrow[TT * h:TT * h + TT, :]).then_inc(m_dma[s], 16)

            for t in range(TT):
                load_tile(0, t)
            for n, w in (("q", wq), ("k", wk), ("v", wv)):
                sp.dma_start(stage[n][:], w.rearrange("(c p) n -> p c n", p=P)).then_inc(w_ld[n], 16)
            sp.dma_start(bo_b[:], bo.rearrange("(a n) -> a n", a=1).to_broadcast([P, D])).then_inc(const_ld, 16)
            sp.dma_start(gate[:, 0:1], g1.rearrange("(a n) -> a n", a=1).to_broadcast([P, 1])).then_inc(const_ld, 16)
            sp.wait_ge(w_ready, 1)
            sp.dma_start(stage["o"][:], wo.rearrange("(c p) n -> p c n", p=P)).then_inc(w_ld["o"], 16)
            u = 3 * TT
            sp.wait_ge(init_done, 2)
            arrange(0, 0, u)
            arrange(0, 1, u + 2)
            max_rows(0, 0)
            unit = Count(PRE_UNITS)

            def step(b, j, r=0):
                known = isinstance(b, int)
                more = not known or b < B - 1
                if j == 0 and known and b == 0:
                    for t in range(TT):
                        load_tile(1, t)
                uq = unit.take() if more or j < 2 else None
                uk = unit.take() if more or j < 2 else None
                w = not known or b > 0
                if w:
                    since(sp, x2_st[j % 2], (b * 2 - 1 + j // 2) * 16)
                    sp.dma_start(xr[:, j % 2, :], xt[b - 1, j]).then_inc(xr_ld[j % 2], 16)
                if uq is not None:
                    arrange(b, j + 2, uq)
                if w:
                    unit.take()
                if more:
                    unit.take(2 if j < 2 else 1)
                if more or j < 3:
                    max_rows(b, j + 1)
                if j == 2 and (not known or b < B - 2):
                    for t in range(TT):
                        load_tile(b + 2, t)
                if w:
                    sp.wait_ge(evacuated, unit.take() + 1)
                    sp.dma_start(x2t_d[b - 1, j], x2t[:, j % 2, :]).then_inc(x2_st[j % 2], 16)
                if more:
                    unit.take(2 if j < 2 else 1)

            batches(sp, lambda b: at_batch(unit, b), step)
            for j in range(4):
                sp.wait_ge(x2_st[j % 2], (B * 2 - 1 + j // 2) * 16)
                sp.dma_start(xr[:, j % 2, :], xt[B - 1, j]).then_inc(xr_ld[j % 2], 16)
                unit.take()
                sp.wait_ge(evacuated, unit.take() + 1)
                sp.dma_start(x2t_d[B - 1, j], x2t[:, j % 2, :]).then_inc(x2_st[j % 2], 16)
            for r in range(2):
                sp.wait_ge(x2_st[r], (B * 2 + 1) * 16)

        @block.gpsimd
        def _(pool):
            links = Count(0)

            def link(ins):
                ins.then_inc(pool_chain, 1)
                pool.wait_ge(pool_chain, links.take() + 1)

            def factors(b):
                pool.wait_ge(stats_ready, (b + 1) * TT)
                layernorm_factors(nc.gpsimd, link, stats, work, ln_cst, rs[:], nb[:], D).then_inc(ln_ready, 1)

            nc.gpsimd.memset(K2[:], 0.0).then_inc(init_done, 1)
            nc.gpsimd.memset(Q2[:], 0.0).then_inc(init_done, 1)
            factors(0)
            nc.gpsimd.memset(V[:, :, :, :, HD:HD + 1], 1.0).then_inc(init_done, 1)
            pool.wait_ge(xn_ready, TT)
            factors(1)
            pool.wait_ge(tanh_done, 1)
            nc.gpsimd.tensor_scalar(tgbo[:], bo_b[:], gate[:, 1:2], None, ALU.mult).then_inc(tgbo_ready, 1)
            pool.wait_ge(tgbo_ready, 1)

            def step(b, j, r=0):
                known = isinstance(b, int)
                if not known or b > 0:
                    k = j % 2
                    pool.wait_ge(xr_ld[k], (b * 2 - 1 + j // 2) * 16)
                    since(pool, x2_st[k], (b * 2 - 1 + j // 2) * 16)
                    nc.gpsimd.tensor_tensor(xb[:, k, :], xr[:, k, :], tgbo[:], ALU.add).then_inc(xb_ready, 1)
                for hh in range(2):
                    hd = b * HB + 2 * j + hh
                    for c in (2, 3):
                        pool.wait_ge(ph_ready, hd * 4 + c + 1)
                        nc.gpsimd.tensor_tensor(Pl[:, hh, c, :], P32[:, c, :], Ph[:, hh, c, :],
                                                ALU.subtract).then_inc(pl_pool, 1)
                if j == 3 and (not known or b < B - 2):
                    factors(b + 2)

            batches(pool, lambda b: links.set(b * LN_CHAIN + 2 * LN_CHAIN, 0), step)
            for j in range(4):
                k = j % 2
                pool.wait_ge(xr_ld[k], (B * 2 - 1 + j // 2) * 16)
                pool.wait_ge(x2_st[k], (B * 2 - 1 + j // 2) * 16)
                nc.gpsimd.tensor_tensor(xb[:, k, :], xr[:, k, :], tgbo[:], ALU.add).then_inc(xb_ready, 1)

        @block.scalar
        def _(act):
            def hi_part(u, dst, scale):
                act.wait_ge(filled, u + 1)
                src = G[:, unit.bank, :]
                if dst.shape[-1] != S:
                    src = src.rearrange("p (c n) -> p c n", c=dst.shape[1])
                nc.scalar.activation(dst, src, ACT.Copy, scale=scale).then_inc(hi_done, 1)

            def normalise(n, t):
                act.wait_ge(ln_ready, n + 1)
                nc.scalar.activation(xn[:, t % 2, :], x_in[:, t, :], ACT.Identity,
                                     scale=rs[:, t:t + 1], bias=nb[:, t:t + 1]).then_inc(xn_ready, 1)

            def v_view(r, t, lo):
                return V[:, r, t, :, (HD + 1 if lo else 0):(2 * HD + 1 if lo else HD)]

            def exps(hd, hh, *chunks):
                for c in chunks:
                    act.wait_ge(st_filled, hd * 4 + c + 1)
                    since(act, pl_vec if c < 2 else pl_pool, hd * 2 + c % 2 - 1)
                    nc.scalar.activation(P32[:, c, :], ST[:, c % 2, :], ACT.Exp,
                                         scale=0.125 / SC2).then_inc(p_ready, 1)
                    since(act, pv_done, hd - 1)
                    nc.scalar.activation(Ph[:, hh, c, :], ST[:, c % 2, :], ACT.Exp,
                                         scale=0.125 / SC2).then_inc(ph_ready, 1)

            def weight_hi(n):
                act.wait_ge(w_ld[n], 16)
                nc.scalar.activation(W[n][0][:], stage[n][:], ACT.Copy, scale=WS).then_inc(w_hi, 1)

            unit = Count(0)

            def transposed(b, t, r):
                for dst, scale in ((xT[r][0], 1.0), (cT[r][0], XS)):
                    hi_part(unit.take(), dst[:, :, t * P:(t + 1) * P], scale)

            for t in range(TT):
                normalise(0, t)
                transposed(0, t, 0)
                weight_hi("qkvo"[t])
            act.wait_ge(const_ld, 32)
            nc.scalar.activation(gate[:, 1:2], gate[:, 0:1], ACT.Tanh).then_inc(tanh_done, 1)
            for t in range(TT):
                u = unit.take()
                act.wait_ge(filled, u + 1)
                nc.scalar.activation(v_view(0, t, False), G[:, unit.bank, :].rearrange("p (h d) -> p h d", d=HD),
                                     ACT.Copy, scale=QS).then_inc(hi_done, 1)
            for pair in range(2):
                for n in "qk":
                    if pair:
                        act.wait_ge(qk_dma[0], QK_DMAS * 16)
                    hi_part(unit.take(), native[n][0][:], QS)

            def step(b, j, r=0):
                known = isinstance(b, int)
                more = not known or b < B - 1
                w = not known or b > 0
                nr = 1 - r
                hd = b * HB + 2 * j

                def project_hi(n):
                    if more or j < 2:
                        s, use = slot_and_use(b, j + 1)
                        act.wait_ge(qk_dma[s], use * QK_DMAS * 16)
                        hi_part(unit.take(), native[n][0][:], QS)

                def side(t):
                    if j < 2:
                        transposed(b, t, nr)
                    else:
                        u = unit.take()
                        act.wait_ge(filled, u + 1)
                        nc.scalar.activation(v_view(nr, t, False), G[:, unit.bank, :].rearrange("p (h d) -> p h d", d=HD),
                                             ACT.Copy, scale=QS).then_inc(hi_done, 1)

                exps(hd, 0, 0, 1)
                project_hi("q")
                exps(hd, 0, 2, 3)
                if more and j < 2:
                    for t in (2 * j, 2 * j + 1):
                        normalise(b + 1, t)
                project_hi("k")
                exps(hd + 1, 1, 0)
                if w:
                    hi_part(unit.take(), oT[0][:], 1.0)
                exps(hd + 1, 1, 1)
                if more:
                    side(2 * (j % 2))
                exps(hd + 1, 1, 2)
                if w:
                    unit.take()
                exps(hd + 1, 1, 3)
                if more:
                    side(2 * (j % 2) + 1)

            batches(act, lambda b: at_batch(unit, b), step)
            for j in range(4):
                hi_part(unit.take(), oT[0][:], 1.0)
                unit.take()

        @block.vector
        def _(dve):
            links = Count(0)

            def link(ins):
                ins.then_inc(chain, 1)
                dve.wait_ge(chain, links.take() + 1)

            unit = Count(0)
            hi = Count(0)

            def lo_part(dst, hi_view, scale):
                u = unit.take()
                dve.wait_ge(hi_done, hi.take() + 1)
                src = G[:, unit.bank, :]
                if dst.shape[-1] != S:
                    src = src.rearrange("p (c n) -> p c n", c=dst.shape[1])
                nc.vector.scalar_tensor_tensor(out=dst, in0=src, scalar=scale, in1=hi_view,
                                               op0=ALU.mult, op1=ALU.subtract).then_inc(evacuated, 1)

            def statistics(t, use):
                dve.wait_ge(x_ld[t], use * 16)
                nc.vector.bn_stats(stats[:, t, :], x_in[:, t, :]).then_inc(stats_ready, 1)

            def row_max(n, k, odd):
                dve.wait_ge(mx_filled, n + 1)
                nc.vector.tensor_reduce(out=mx[:, k // TT, k % TT:k % TT + 1], in_=MX[:, (k + odd) % 2, :], axis=AXX,
                                        op=ALU.max).then_inc(mx_taken, 1)

            def negate(n):
                dve.wait_ge(mx_taken, n)
                nc.vector.tensor_scalar(mneg[:], mx[:].rearrange("p h t -> p (h t)"), -1.0 / SC2, SHIFT,
                                        ALU.mult, ALU.add).then_inc(mneg_ready, 1)

            def max_rows(n, odd):
                dve.wait_ge(mx_filled, n + 1)
                nc.vector.tensor_copy(mrow[:], MX[0:2 * TT, odd, 0:P]).then_inc(mrow_ready, 1)

            def transposed(t, r):
                for (hi_t, lo_t), scale in ((xT[r], 1.0), (cT[r], XS)):
                    c = slice(t * P, (t + 1) * P)
                    lo_part(lo_t[:, :, c], hi_t[:, :, c], scale)

            def v_lo(t, r):
                u = unit.take()
                dve.wait_ge(hi_done, hi.take() + 1)
                nc.vector.scalar_tensor_tensor(
                    out=V[:, r, t, :, HD + 1:], in0=G[:, unit.bank, :].rearrange("p (h d) -> p h d", d=HD), scalar=QS,
                    in1=V[:, r, t, :, 0:HD], op0=ALU.mult, op1=ALU.subtract).then_inc(evacuated, 1)

            def head_out(hd, j, hh, r):
                dve.wait_ge(pv_done, hd + 1)
                link(nc.vector.reciprocal(rec[:, hh, :], PV[:, hh, :, HD:HD + 1].rearrange("p t o -> p (t o)")))
                h = 2 * j + hh
                nc.vector.tensor_tensor(O[r][:, :, h * HD:(h + 1) * HD], PV[:, hh, :, 0:HD],
                                        rec[:, hh, :].unsqueeze(2).to_broadcast([P, TT, HD]),
                                        ALU.mult).then_inc(o_ready, 1)

            def probs_lo(hd, hh, c):
                dve.wait_ge(ph_ready, hd * 4 + c + 1)
                nc.vector.tensor_tensor(Pl[:, hh, c, :], P32[:, c, :], Ph[:, hh, c, :],
                                        ALU.subtract).then_inc(pl_vec, 1)

            def x2_rows(w, j, uses):
                u = unit.take()
                dve.wait_ge(filled, u + 1)
                dve.wait_ge(xb_ready, w + 1)
                since(dve, x2_st[j % 2], uses)
                nc.vector.scalar_tensor_tensor(out=x2t[:, j % 2, :], in0=G[:, unit.bank, :], scalar=gate[:, 2:3],
                                               in1=xb[:, j % 2, :], op0=ALU.mult, op1=ALU.add).then_inc(evacuated, 1)
                dve.wait_ge(evacuated, u + 1)
                nc.vector.bn_stats(row_stats[:], x2t[:, j % 2, :]).then_inc(row_stats_ready, 1)
                dve.wait_ge(row_stats_ready, w + 1)
                nc.vector.tensor_scalar(x2_stats[:, w, :], row_stats[:], 1.0, None, ALU.mult)

            def weight_lo(n, k):
                dve.wait_ge(w_hi, k + 1)
                nc.vector.scalar_tensor_tensor(out=W[n][1][:].rearrange("p c n -> p (c n)"),
                                               in0=stage[n][:].rearrange("p c n -> p (c n)"), scalar=WS,
                                               in1=W[n][0][:].rearrange("p c n -> p (c n)"),
                                               op0=ALU.mult, op1=ALU.subtract).then_inc(w_ready, 1)

            for t in range(TT):
                statistics(t, 1)
            for t in range(TT):
                transposed(t, 0)
                weight_lo("qkvo"[t], t)
            dve.wait_ge(init_done, 3)
            for h, row in ((0, HD), (1, 0)):
                nc.vector.memset(K2[row:row + 1, :, h, :], SC2).then_inc(init_done, 1)
            dve.wait_ge(tanh_done, 1)
            nc.vector.tensor_scalar(gate[:, 2:3], gate[:, 1:2], 1.0 / (XS * WS), None, ALU.mult).then_inc(gate_ready, 1)
            dve.wait_ge(gate_ready, 1)
            for t in range(TT):
                v_lo(t, 0)
            for pair in range(2):
                for n in "qk":
                    lo_part(native[n][1][:], native[n][0][:], QS)
            for k in range(8):
                row_max(k, k, 0)
            negate(8)
            max_rows(8, 0)
            for t in range(TT):
                statistics(t, 2)

            def step(b, j, r=0):
                known = isinstance(b, int)
                more = not known or b < B - 1
                w = not known or b > 0
                nr = 1 - r
                hd = b * HB + 2 * j
                mxn = (b * PAIRS + (j + 1)) * MX_UNITS
                odd = (j + 1) % 2
                nmax = more or j < 3

                def maxima(*ks):
                    for k in ks:
                        if nmax:
                            row_max(mxn + k, k, odd)

                def side(t):
                    transposed(t, nr) if j < 2 else v_lo(t, nr)

                def proj_lo(n):
                    if more or j < 2:
                        lo_part(native[n][1][:], native[n][0][:], QS)

                maxima(0, 1, 2, 3)
                probs_lo(hd, 0, 0)
                proj_lo("q")
                maxima(4, 5)
                probs_lo(hd, 0, 1)
                maxima(6, 7)
                if nmax:
                    negate((b * PAIRS + (j + 2)) * (2 * TT))
                proj_lo("k")
                if w or j:
                    head_out(hd - 1, (j - 1) % 4, 1, r if j else nr)
                if nmax:
                    max_rows(mxn + 8, odd)
                if w:
                    lo_part(oT[1][:], oT[0][:], 1.0)
                probs_lo(hd + 1, 1, 0)
                if more:
                    side(2 * (j % 2))
                if j == 3 and (not known or b < B - 2):
                    for t in range(TT):
                        statistics(t, b + 3)
                probs_lo(hd + 1, 1, 1)
                if w:
                    x2_rows(b * 4 - 4 + j, j, (b * 2 - 1 + j // 2) * 16)
                head_out(hd, j, 0, r)
                if more:
                    side(2 * (j % 2) + 1)

            def at_counts(b):
                at_batch(unit, b)
                hi.value = b * BATCH_HI + (PRE_HI - 4)
                links.value = b * HB + (-1)

            batches(dve, at_counts, step)
            head_out(B * HB - 1, 3, 1, (B - 1) % 2)
            for j in range(4):
                lo_part(oT[1][:], oT[0][:], 1.0)
                x2_rows(B * 4 - 4 + j, j, (B * 2 - 1 + j // 2) * 16)

        @block.tensor
        def _(pe):
            unit = Count(0)

            def bank():
                u = unit.take()
                since(pe, evacuated, u - 1)
                return u, G[:, unit.bank, :]

            def product(out, parts, n0=0, n1=None):
                n1 = len(parts) if n1 is None else n1
                for n in range(n0, n1):
                    a, m = parts[n]
                    last = nc.tensor.matmul(out, a, m, start=(n == 0), stop=(n == len(parts) - 1))
                return last

            def split_parts(stat, mov):
                return [(stat(a, c), mov(m, c)) for c in range(KC) for a, m in ((0, 0), (0, 1), (1, 0))]

            def transposes(src):
                u, g = bank()
                for c in range(KC):
                    last = nc.tensor.transpose(g[:, c * P:(c + 1) * P], src[:, c * P:(c + 1) * P], ident[:])
                last.then_inc(filled, 1)

            def x_tile(t, n):
                pe.wait_ge(xn_ready, n + 1)
                transposes(xn[:, t % 2, :])

            def c_tile(t, use):
                pe.wait_ge(c_ld[t], use * 16)
                transposes(c_in[:, t, :])

            def qk_parts(n, pair, r):
                act_t = xT[r] if n == "q" else cT[r]
                return split_parts(lambda a, c: W[n][a][:, c, pair * P:(pair + 1) * P],
                                   lambda m, c: act_t[m][:, c, :])

            def v_parts(t, r):
                return split_parts(lambda a, c: cT[r][a][:, c, t * P:(t + 1) * P], lambda m, c: W["v"][m][:, c, :])

            def row_max_scores(n, k, s, use, odd, pair):
                h, t = k // TT, k % TT
                if k == 0:
                    pe.wait_ge(qk_dma[s], use * QK_DMAS * 16)
                if k == 1:
                    since(pe, mrow_ready, pair)
                else:
                    since(pe, mx_taken, pair * (2 * TT) + k - (1 if k > 1 else 0))
                nc.tensor.matmul(MX[:, (k + odd) % 2, :], Q1[:, s, h, t * P:(t + 1) * P], K1[:, s, h, :],
                                 start=True, stop=True).then_inc(mx_filled, 1)

            def max_transpose(pair, odd):
                pe.wait_ge(mneg_ready, pair + 1)
                nc.tensor.transpose(MX[0:2 * TT, odd, 0:P], mneg[:], ident[:]).then_inc(mx_filled, 1)

            def scores(b, j, k):
                hh, c = divmod(k, TT)
                n = b * (HB * TT) + 8 * j + k
                if k == 0:
                    pe.wait_ge(m_dma[j], (b + 1) * 32)
                since(pe, ph_ready, n - 1)
                cols = slice(c * P, (c + 1) * P)
                nc.tensor.matmul(ST[:, c % 2, :], K1[:, j, hh, cols], Q1[:, j, hh, :], start=True, stop=False)
                nc.tensor.matmul(ST[:, c % 2, :], K2[:, j, hh, cols], Q2[:, j, hh, :],
                                 start=False, stop=True).then_inc(st_filled, 1)

            def weighted(hd, h, r, t):
                hh = h % 2
                if t == 0:
                    pe.wait_ge(pl_vec, hd * 2 + 2)
                    pe.wait_ge(pl_pool, hd * 2 + 2)
                    since(pe, o_ready, hd - 1)
                cols = slice(t * P, (t + 1) * P)
                out = PV[:, hh, t, :]
                for c in range(TT):
                    nc.tensor.matmul(out[:, 0:HD + 1], Ph[:, hh, c, cols], V[:, r, c, h, 0:HD + 1],
                                     start=(c == 0), stop=False)
                    nc.tensor.matmul(out[:, 0:HD], Ph[:, hh, c, cols], V[:, r, c, h, HD + 1:],
                                     start=False, stop=False)
                    last = nc.tensor.matmul(out[:, 0:HD + 1], Pl[:, hh, c, cols], V[:, r, c, h, 0:HD + 1],
                                            start=False, stop=(c == TT - 1))
                if t == TT - 1:
                    last.then_inc(pv_done, 1)

            def out_project(split):
                u, g = bank()
                pe.wait_ge(evacuated, split + 1)
                product(g, split_parts(lambda a, c: oT[a][:, c, :],
                                       lambda m, c: W["o"][m][:, c, :])).then_inc(filled, 1)

            for t in range(TT):
                x_tile(t, t)
                c_tile(t, 1)
            pe.wait_ge(w_ready, 3)
            pe.wait_ge(evacuated, 2 * TT)
            for t in range(TT):
                u, g = bank()
                product(g, v_parts(t, 0)).then_inc(filled, 1)
            for pair in range(2):
                for n in "qk":
                    u, g = bank()
                    product(g, qk_parts(n, pair, 0)).then_inc(filled, 1)
            for k in range(8):
                row_max_scores(k, k, 0, 1, 0, 0)
            max_transpose(0, 0)
            pe.wait_ge(init_done, 5)
            pe.wait_ge(w_ready, 4)

            def step(b, j, r=0):
                known = isinstance(b, int)
                more = not known or b < B - 1
                w = not known or b > 0
                nr = 1 - r
                hd = b * HB + 2 * j
                odd = (j + 1) % 2
                s, use = slot_and_use(b, j + 1)
                qk_r = r if j < 2 else nr

                def maxima(*ks):
                    for k in ks:
                        if more or j < 3:
                            row_max_scores(0, k, s, use, odd, b * PAIRS + (j + 1))

                proj = more or j < 2
                parts = {n: qk_parts(n, (j + 2) % 4, qk_r) for n in "qk"}

                def side(t):
                    if j < 2:
                        x_tile(t, b * 4 + 4 + t)
                        c_tile(t, b + 2)
                    else:
                        u, g = bank()
                        product(g, v_parts(t, nr)).then_inc(filled, 1)

                def last_head(*ts):
                    for t in ts:
                        if w or j:
                            weighted(hd - 1, (2 * j - 1) % HB, r if j else nr, t)

                for k in range(4):
                    n = "qk"[k // 2]
                    scores(b, j, k)
                    maxima(2 * k)
                    if proj and k % 2 == 0:
                        u, g = bank()
                        if j == 2 and k == 0:
                            pe.wait_ge(evacuated, u)
                        product(g, parts[n], 0, 6)
                    maxima(2 * k + 1)
                    if k % 2 == 0:
                        last_head(k // 2)
                    if proj and k % 2 == 1:
                        product(g, parts[n], 6).then_inc(filled, 1)
                scores(b, j, 4)
                last_head(2, 3)
                if w:
                    pe.wait_ge(o_ready, b * HB)
                    split = unit.value
                    transposes(O[nr][:, j, :])
                if more or j < 3:
                    max_transpose(b * PAIRS + j + 1, odd)
                scores(b, j, 5)
                if more:
                    side(2 * (j % 2))
                scores(b, j, 6)
                weighted(hd, 2 * j, r, 0)
                weighted(hd, 2 * j, r, 1)
                if w:
                    out_project(split)
                scores(b, j, 7)
                weighted(hd, 2 * j, r, 2)
                weighted(hd, 2 * j, r, 3)
                if more:
                    side(2 * (j % 2) + 1)

            batches(pe, lambda b: at_batch(unit, b), step)
            for t in range(TT):
                weighted(B * HB - 1, HB - 1, (B - 1) % 2, t)
            pe.wait_ge(o_ready, B * HB)
            for j in range(4):
                split = unit.value
                transposes(O[(B - 1) % 2][:, j, :])
                out_project(split)


def ffn_phase(nc, x2_dram, x2_stats, g2, gate_w, wu, wv, wo, out, ident, ln_cst):
    B, S, D = x2_dram.shape
    E, _, R = wu.shape
    KC = D // P
    TT = S // P
    K = 2
    ROWS = B * S
    UR = 2 * P
    TU = UR // P
    FU = KC * TU // TT
    UNITS = ROWS * K // UR + E - 1
    LISTED = UNITS + 2
    SPARE = LISTED - ROWS * K // UR
    BE = ROWS // UR
    BLOCKS = E * BE + SPARE
    TK = TT * K
    x2_d = x2_dram.rearrange("b (t p) d -> b p t d", p=P)
    out_d = out.rearrange("b (h t p) d -> (b h) p t d", t=2, p=P)
    RING, PAIRS = 4, ROWS // P // 2
    xn_dram = nc.dram_tensor("xn_scratch", (ROWS, D), F32, kind="Internal").ap()
    xn_d = xn_dram.rearrange("(b t p) d -> b p t d", t=TT, p=P)
    ids_dram = nc.dram_tensor("row_number_table", (BLOCKS * UR, 1), U32, kind="Internal").ap()
    ids_d = ids_dram.rearrange("(s p k) o -> s p (k o)", p=P, k=TU)
    y_dram = nc.dram_tensor("result_table", (UNITS * UR, D), F32, kind="Internal").ap()
    y_d = y_dram.rearrange("(s p k) d -> s p k d", p=P, k=TU)

    ctx = ExitStack()
    with ctx:
        sb = lambda name, shape, dt=F32: ctx.enter_context(nc.sbuf_tensor(name, shape, dt))
        ps = lambda name, shape, dt=F32: ctx.enter_context(nc.psum_tensor(name, shape, dt))
        sem = lambda name: ctx.enter_context(nc.semaphore(name))
        stage = {n: sb(f"f{n}_stage", [P, E, D]) for n in "uvo"}
        g_stage = sb("gate_w_stage", [P, KC, E])
        W = {n: (sb(f"f{n}_hi", [P, E, D], F16), sb(f"f{n}_lo", [P, E, D], F16)) for n in "uvo"}
        Wg = (sb("fg_hi", [P, KC, E], F16), sb("fg_lo", [P, KC, E], F16))
        halves = lambda z: z[:].rearrange("p (r t) d -> p r t d", r=2)
        xg, y_sb = halves(stage["u"]), halves(stage["v"])
        yg = lambda q: stage["ou"[q // 2]][:, q % 2 * 2 * K:(q % 2 + 1) * 2 * K, :]
        res = lambda q: stage["v"][:, 2 * q:2 * q + 2, :]
        x2s = sb("x2s", [P, B, TT, D])
        xn = sb("xn2", [P, 2, TT, D])
        xT = (sb("x2T_hi", [P, 2, KC, S], F16), sb("x2T_lo", [P, 2, KC, S], F16))
        th = sb("th", [P, S])
        s32 = sb("s32", [P, S])
        sT = (sb("sT_hi", [P, S], F16), sb("sT_lo", [P, S], F16))
        work = sb("work2", [P, 6, B * TT])
        rs = sb("rs2", [P, B * TT])
        nb = sb("nb2", [P, B * TT])
        lg = sb("lg", [P, TT, E])
        top = sb("top", [P, TT, 8])
        took = sb("took", [P, 1])
        idx = sb("idx", [P, TT, 8], U32)
        idf = sb("idf", [P, TT, K])
        gap = sb("gap", [P, TT])
        gexp = sb("gexp", [P, TT])
        den = sb("den", [P, TT])
        w12 = sb("w12", [P, TT, K])
        w_all = sb("w_all", [P, B * TK])
        chosen = sb("chosen", [P, TT, K, E])
        both = sb("both", [P, TT, E], F16)
        rank = sb("rank", [P, TT, E])
        place = sb("place", [P, TT, K, E])
        pos_f = sb("pos_f", [P, TK])
        pos_st = sb("pos_staged", [P, 2, TK], U32)
        tok_st = sb("row_numbers_staged", [P, 2, TT], U32)
        pos_all = sb("pos_all", [P, B * TK])
        y_cmp = th[:, 0:B * TK * (E - 1)].rearrange("p (n e) -> p n e", e=E - 1)
        y_off = sb("y_off", [P, B * TK])
        y_step = sb("y_step", [P, E - 1])
        y_pos = sb("y_pos", [P, B * TK], U32)
        tokid = sb("tokid", [P, B * TT], U32)
        base = sb("base", [P, E])
        start0 = sb("start0", [P, E])
        tri = sb("tri", [P, P], F16)
        ones = sb("ones", [P, P], F16)
        tri32 = th[:, 0:P]
        ones32 = sb("ones32", [P, P])
        iota = sb("iota", [P, E])
        thr = sb("thr", [P, BE])
        unit_no = sb("unit_no", [P, LISTED])
        cmp = sb("cmp", [P, E, BE])
        nt = sb("nt", [P, E])
        cum = sb("cum", [P, 4, E])
        ucmp, ucmp2 = (z[:, 0:LISTED * E].rearrange("p (u e) -> p u e", e=E) for z in (s32, th))
        ue = sb("ue", [P, LISTED])
        uw = sb("uw", [P, 2, LISTED])
        unit_expert = sb("unit_expert", [P, LISTED], U32)
        unit_block = sb("unit_block", [P, LISTED], U32)
        zeros = s32[:, 0:BLOCKS * UR // P // TU].bitcast(U32)
        unit_rows = sb("unit_row_numbers", [P, LISTED * TU], U32)
        rows_st = sb("unit_rows_staged", [P, 2, TU], U32)
        junk = sb("junk", [P, 1])
        gate = sb("gate2", [P, 3])

        U = ps("U", [P, S])
        Vp = ps("Vp", [P, S])
        M = ps("M", [P, 2, S])
        Y = ps("Y", [P, TT, D])
        L, RK = U, Vp

        g_ld = sem("gate_w_loaded")
        w_ld = {n: sem(f"f{n}_loaded") for n in "uvo"}
        const_ld = sem("f_constants_loaded")
        consts = sem("f_constants_written")
        tanh_done, gate_ready = sem("f_tanh_done"), sem("f_gate_ready")
        w_hi, w_ready = sem("f_weight_hi"), sem("f_weights_ready")
        x_ld = [sem(f"x2_loaded{r}") for r in range(2)]
        xn_st = [sem(f"xn_stored{r}") for r in range(2)]
        zero_st = sem("table_cleared")
        chain, pool_chain, held = sem("f_vector_chain"), sem("f_pool_chain"), sem("pool_held")
        y_pos_ready = sem("result_places_ready")
        ln_ready, xn_ready = sem("f_ln_ready"), sem("f_xn_ready")
        m_filled, t_hi, m_free = sem("transposes_filled"), sem("xT_hi_written"), sem("transposes_taken")
        l_filled, l_free = sem("logits_filled"), sem("logits_taken")
        gap_ready, exp_ready = sem("logit_gap_ready"), sem("gap_exp_ready")
        both_ready, rk_filled, pos_ready = sem("choices_ready"), sem("ranks_filled"), sem("places_ready")
        scattered = [sem(f"row_numbers_scattered{r}") for r in range(2)]
        table_ready = sem("unit_table_ready")
        rows_ld = [sem(f"unit_rows_loaded{r}") for r in range(2)]
        xg_ld = [sem(f"rows_gathered{r}") for r in range(2)]
        u_filled, v_filled = sem("u_filled"), sem("v_filled")
        tanh_ready, a_done, s_done = sem("tanh_ready"), sem("u_bank_free"), sem("v_bank_free")
        s_hi, s_lo = sem("sT_hi_written"), sem("sT_lo_written")
        y_filled, y_taken = sem("y_tiles_done"), sem("y_tiles_taken")
        y_st = [sem(f"y_stored{r}") for r in range(2)]
        yg_ld = [sem(f"results_gathered{q}") for q in range(RING)]
        half_done, out_ready = sem("first_results_added"), sem("out_ready")
        st = [sem(f"out_stored{q}") for q in range(RING)]
        block = ctx.enter_context(nc.Block())

        def groups(eng, group):
            group(0, 0, 0)
            group(1, 1, 0)
            with eng.Fori(1, B // 2 - 1) as i:
                group(i * 2, 0, i)
                group(i * 2 + 1, 1, i)
            group(B - 2, 0, B // 2 - 1)
            group(B - 1, 1, B // 2 - 1)

        def units(eng, unit):
            unit(0, 0, 0)
            unit(1, 1, 0)
            with eng.Fori(1, (UNITS - 1) // 2) as i:
                unit(i * 2, 0, i)
                unit(i * 2 + 1, 1, i)
            for s in range((UNITS - 1) // 2 * 2, UNITS):
                unit(s, s % 2, s // 2)

        def pairs(eng, pair):
            for q in range(RING):
                pair(q, q, 0)
            with eng.Fori(1, PAIRS // RING - 1) as i:
                for q in range(RING):
                    pair(i * RING + q, q, i)
            for q in range(RING):
                pair(PAIRS - RING + q, q, PAIRS // RING - 1)

        x2_rows = x2s[:].rearrange("p b t d -> p (b t) d")
        place_st = lambda q: pos_st[:].rearrange("p r k -> p (r k)")[:, q * 2 * K:(q + 1) * 2 * K]
        known = lambda v: isinstance(v, int)

        PARTS = 4
        part = lambda z, k: z[:, k * (E // PARTS):(k + 1) * (E // PARTS), :]
        route_bank = lambda c: Y[:, c, :]
        unit_bank = lambda c: M[:, c % 2, :]

        def cols(z, f, n):
            return z[:, f * n:(f + 1) * n] if known(f) else z[:, bass.ds(f * n, n)]

        @block.sync
        def _(sp):
            for f in range(2):
                sp.dma_start(x2s[:, f], x2_d[f]).then_inc(x_ld[f], 16)
            sp.dma_start(g_stage[:], gate_w.rearrange("(c p) e -> p c e", p=P)).then_inc(g_ld, 16)
            sp.dma_start(gate[:, 0:1], g2.rearrange("(a n) -> a n", a=1).to_broadcast([P, 1])).then_inc(const_ld, 16)
            for r in range(2):
                sp.sem_inc(y_st[r], 16)
            sp.wait_ge(consts, 1)
            for t in range(TU):
                sp.dma_start(ids_dram.rearrange("(t p k) o -> t p (k o)", t=TU, p=P)[t], zeros).then_inc(zero_st, 16)

            def group(f, r, half):
                sp.wait_ge(xn_ready, f + 1)
                sp.dma_start(xn_d[f], xn[:, r]).then_inc(xn_st[r], 16)
                if not known(f) or f < B - 2:
                    sp.dma_start(x2s[:, f + 2],
                                 x2_d[f + 2]).then_inc(x_ld[r], 16)
                if known(f) and f >= B - 2:
                    for e in range(E):
                        for n, w in ((("u", wu),) if f == B - 2 else (("v", wv), ("o", wo))):
                            if n == "o":
                                dst, src = stage[n][:, e, :], w[e]
                            else:
                                dst = stage[n][:, e, :].rearrange("p (c r) -> p c r", c=KC)
                                src = w[e].rearrange("(c p) r -> p c r", p=P)
                            sp.dma_start(dst, src).then_inc(w_ld[n], 16)

            groups(sp, group)

            def row_numbers(s, r, use=0):
                block_no = sp.value_load(cols(unit_block, s, 1)[0:1], min_val=0, max_val=BLOCKS - 1)
                since(sp, rows_ld[r], use * 16)
                sp.dma_start(cols(unit_rows, s, TU), ids_d[block_no]).then_inc(rows_ld[r], 16)

            def store(s, r):
                sp.wait_ge(y_taken, s * TU + TU)
                sp.dma_start(y_d[s], y_sb[:, r, 0:TU]).then_inc(y_st[r], 16)

            for r in range(2):
                sp.wait_ge(scattered[r], B // 2 * TK * 16)
            sp.wait_ge(table_ready, 2)
            row_numbers(0, 0)
            row_numbers(1, 1)

            def unit(s, r, half):
                if not known(s) or s < UNITS - 2:
                    row_numbers(s + 2, r, half + 1)
                if not known(s) or s > 1:
                    store(s - 2, r)

            units(sp, unit)
            store(UNITS - 2, (UNITS - 2) % 2)
            store(UNITS - 1, (UNITS - 1) % 2)

            def result(g, q, use):
                sp.wait_ge(out_ready, g + 1)
                sp.dma_start(out_d[g], res(q)).then_inc(st[q], 16)

            pairs(sp, result)
            for q in range(RING):
                sp.wait_ge(st[q], PAIRS // RING * 16)

        @block.gpsimd
        def _(pool):
            links = Count(0)

            def link(ins):
                ins.then_inc(pool_chain, 1)
                pool.wait_ge(pool_chain, links.take() + 1)

            def hold(n):
                since(pool, held, n)
                nc.gpsimd.tensor_tensor(junk[:], ones32[:, 0:1], ones32[:, 0:1], ALU.mult).then_inc(held, 1)

            def scatter(f, r):
                pool.wait_ge(pos_ready, f + 1)
                hold(f)
                for j in range(TK):
                    nc.gpsimd.indirect_dma_start(ids_dram, bass.IndirectOffsetOnAxis(pos_st[:, r, j:j + 1], 0),
                                                 tok_st[:, r, j // K:j // K + 1], None).then_inc(scattered[r], 16)

            layernorm_factors(nc.gpsimd, link, x2_stats, work, ln_cst, rs[:], nb[:], D).then_inc(ln_ready, 1)
            nc.gpsimd.iota(iota[:], [[1, E]], base=0, channel_multiplier=0,
                           allow_small_or_imprecise_dtypes=True)
            nc.gpsimd.iota(start0[:], [[ROWS, E]], base=0, channel_multiplier=0,
                           allow_small_or_imprecise_dtypes=True)
            nc.gpsimd.iota(thr[:], [[UR, BE]], base=0, channel_multiplier=0,
                           allow_small_or_imprecise_dtypes=True)
            nc.gpsimd.iota(unit_no[:], [[1, LISTED]], base=0, channel_multiplier=0,
                           allow_small_or_imprecise_dtypes=True)
            nc.gpsimd.iota(tokid[:], [[P, B * TT]], base=0, channel_multiplier=1)
            nc.gpsimd.memset(zeros, 0).then_inc(consts, 1)
            nc.gpsimd.memset(ones32[:], 1.0).then_inc(consts, 1)
            pool.wait_ge(consts, 2)
            nc.gpsimd.affine_select(out=tri32, in_=ones32[:], compare_op=ALU.is_gt, fill=0.0, base=0,
                                    pattern=[[1, P]], channel_multiplier=-1).then_inc(consts, 1)
            pool.wait_ge(zero_st, TU * 16)

            def group(f, r, half):
                if not known(f) or f > 0:
                    scatter(f - 1, 1 - r)

            groups(pool, group)
            scatter(B - 1, 1)

            def gather(s, r, half):
                links.set(s + LN_CHAIN, 0)
                since(pool, m_filled, s * FU + (B * KC - FU))
                pool.wait_ge(rows_ld[r], half * 16 + 16)
                link(nc.gpsimd.tensor_copy(rows_st[:, r], cols(unit_rows, s, TU)))
                hold(s + B)
                for t in range(TU):
                    nc.gpsimd.indirect_dma_start(xg[:, r, t, :], None, xn_dram,
                                                 bass.IndirectOffsetOnAxis(rows_st[:, r, t:t + 1], 0)).then_inc(xg_ld[r], 16)

            for r in range(2):
                pool.wait_ge(xn_st[r], B // 2 * 16)
            pool.wait_ge(w_ready, 1 + PARTS)
            units(pool, gather)

            def pair(g, q, use):
                links.set(g + (LN_CHAIN + UNITS), 0)
                since(pool, out_ready, g + (1 - RING))
                link(nc.gpsimd.tensor_copy(place_st(q), cols(y_pos, g, 2 * K)))
                hold(g + (B + UNITS))
                for j in range(2 * K):
                    nc.gpsimd.indirect_dma_start(yg(q)[:, j, :], None, y_dram, bass.IndirectOffsetOnAxis(
                        place_st(q)[:, j:j + 1], 0)).then_inc(yg_ld[q], 16)

            pool.wait_ge(y_pos_ready, 1)
            pool.wait_ge(y_st[0], ((UNITS + 1) // 2 + 1) * 16)
            pool.wait_ge(y_st[1], (UNITS // 2 + 1) * 16)
            pairs(pool, pair)

        @block.scalar
        def _(act):
            def normalise(f, r, half):
                act.wait_ge(x_ld[r], half * 16 + 16)
                since(act, xn_st[r], half * 16)
                for t in range(TT):
                    last = nc.scalar.activation(xn[:, r, t, :], x2s[:, f][:, t, :], ACT.Identity,
                                                scale=cols(rs, f * TT + t, 1), bias=cols(nb, f * TT + t, 1))
                last.then_inc(xn_ready, 1)

            def transposed_hi(q, r, c, bank):
                act.wait_ge(m_filled, q + (c + 1))
                nc.scalar.activation(xT[0][:, r, c, :], bank(c), ACT.Copy).then_inc(t_hi, 1)

            def gap_exp(f):
                act.wait_ge(gap_ready, f + 1)
                nc.scalar.activation(gexp[:], gap[:], ACT.Exp).then_inc(exp_ready, 1)

            act.wait_ge(g_ld, 16)
            nc.scalar.activation(Wg[0][:], g_stage[:], ACT.Copy, scale=WS).then_inc(w_hi, 1)
            act.wait_ge(const_ld, 16)
            nc.scalar.activation(gate[:, 1:2], gate[:, 0:1], ACT.Tanh).then_inc(tanh_done, 1)
            act.wait_ge(ln_ready, 1)
            normalise(0, 0, 0)

            def group(f, r, half):
                for c in range(KC):
                    transposed_hi(f * KC, r, c, route_bank)
                    if c == 1 and (not known(f) or f > 0):
                        gap_exp(f - 1)
                if not known(f) or f < B - 1:
                    normalise(f + 1, 1 - r, half + r)

            groups(act, group)
            gap_exp(B - 1)
            for n in "uvo":
                act.wait_ge(w_ld[n], E * 16)
                for k in range(PARTS):
                    nc.scalar.activation(part(W[n][0], k), part(stage[n], k), ACT.Copy, scale=WS).then_inc(w_hi, 1)
            for c in range(FU):
                transposed_hi(B * KC, 0, c, unit_bank)

            def results(s, r, half):
                act.wait_ge(y_st[r], half * 16 + 16)
                for t in range(TU):
                    act.wait_ge(y_filled, s * TU + (t + 1))
                    nc.scalar.activation(y_sb[:, r, t, :], Y[:, r * TU + t, :], ACT.Copy).then_inc(y_taken, 1)

            def unit(s, r, half):
                act.wait_ge(u_filled, s + 1)
                nc.scalar.activation(th[:, 0:UR], U[:, 0:UR], ACT.Tanh, scale=0.5 / (XS * WS)).then_inc(tanh_ready, 1)
                more = not known(s) or s < UNITS - 1
                if more:
                    for c in range(FU):
                        transposed_hi(s * FU + (B * KC + FU), 1 - r, c, unit_bank)
                act.wait_ge(s_done, s + 1)
                since(act, y_filled, (s - 1) * TU)
                nc.scalar.activation(sT[0][:, r * UR:(r + 1) * UR], s32[:, 0:UR], ACT.Copy).then_inc(s_hi, 1)
                if not known(s) or s > 0:
                    results(s - 1, 1 - r, half - (1 - r))

            units(act, unit)
            results(UNITS - 1, (UNITS - 1) % 2, (UNITS - 1) // 2)

        @block.vector
        def _(dve):
            links = Count(0)

            def link(ins):
                ins.then_inc(chain, 1)
                dve.wait_ge(chain, links.take() + 1)

            def low(src, hi, lo):
                return nc.vector.scalar_tensor_tensor(out=lo, in0=src, scalar=WS, in1=hi, op0=ALU.mult,
                                                      op1=ALU.subtract).then_inc(w_ready, 1)

            def transposed_lo(q, r, c, bank):
                dve.wait_ge(t_hi, q + (c + 1))
                nc.vector.tensor_tensor(xT[1][:, r, c, :], bank(c), xT[0][:, r, c, :],
                                        ALU.subtract).then_inc(m_free, 1)

            def best_two(f):
                dve.wait_ge(l_filled, f + 1)
                nc.vector.tensor_scalar(lg[:].rearrange("p t e -> p (t e)"), L[:, 0:TT * E], 1.0 / (XS * WS), None,
                                        ALU.mult).then_inc(l_free, 1)
                dve.wait_ge(l_free, f + 1)
                nc.vector.tensor_copy(took[:], lg[:, 0, 0:1])
                for t in range(TT):
                    last = nc.vector.max(top[:, t, :], lg[:, t, :])
                link(last)
                nc.vector.tensor_tensor(gap[:], top[:, :, 1:2].rearrange("p t o -> p (t o)"),
                                        top[:, :, 0:1].rearrange("p t o -> p (t o)"), ALU.subtract).then_inc(gap_ready, 1)
                for t in range(TT):
                    last = nc.vector.max_index(idx[:, t, :], top[:, t, :], lg[:, t, :])
                link(last)
                link(nc.vector.tensor_copy(idf[:], idx[:, :, 0:K]))
                link(nc.vector.tensor_tensor(chosen[:].rearrange("p t k e -> p (t k) e"),
                                             iota[:].unsqueeze(1).to_broadcast([P, TK, E]),
                                             idf[:].rearrange("p t k -> p (t k)").unsqueeze(2).to_broadcast([P, TK, E]),
                                             ALU.is_equal))
                nc.vector.tensor_tensor(both[:], chosen[:, :, 0, :], chosen[:, :, 1, :], ALU.add).then_inc(both_ready, 1)

            def places(f, r, half):
                dve.wait_ge(exp_ready, f + 1)
                link(nc.vector.tensor_scalar(den[:], gexp[:], 1.0, None, ALU.add))
                first, second = (w12[:, :, k:k + 1].rearrange("p t o -> p (t o)") for k in range(K))
                link(nc.vector.reciprocal(first, den[:]))
                link(nc.vector.tensor_tensor(second, gexp[:], first, ALU.mult))
                nc.vector.tensor_scalar(cols(w_all, f, TK), w12[:].rearrange("p t k -> p (t k)"), gate[:, 2:3], None, ALU.mult)
                dve.wait_ge(rk_filled, f + 1)
                link(nc.vector.tensor_tensor(rank[:], RK[:, 0:TT * E].rearrange("p (t e) -> p t e", e=E),
                                        base[:].unsqueeze(1).to_broadcast([P, TT, E]), ALU.add))
                nc.vector.tensor_tensor(base[:], base[:], RK[:, TT * E:(TT + 1) * E], ALU.add)
                for k in range(K):
                    last = nc.vector.tensor_tensor(place[:, :, k, :], chosen[:, :, k, :], rank[:], ALU.mult)
                link(last)
                link(nc.vector.tensor_reduce(pos_f[:], place[:].rearrange("p t k e -> p (t k) e"), AXX, ALU.add))
                if r == 0:
                    since(dve, scattered[0], half * (TK * 16))
                nc.vector.tensor_copy(cols(pos_all, f, TK), pos_f[:])
                nc.vector.tensor_copy(pos_st[:, r], pos_f[:])
                nc.vector.tensor_copy(tok_st[:, r], cols(tokid, f, TT)).then_inc(pos_ready, 1)

            def unit_table():
                spread_e = lambda z: z.unsqueeze(1).to_broadcast([P, LISTED, E])
                spread_u = lambda z: z.unsqueeze(2).to_broadcast([P, LISTED, E])
                link(nc.vector.tensor_tensor(nt[:], base[:], start0[:], ALU.subtract))
                link(nc.vector.tensor_tensor(cmp[:], nt[:].unsqueeze(2).to_broadcast([P, E, BE]),
                                             thr[:].unsqueeze(1).to_broadcast([P, E, BE]), ALU.is_gt))
                link(nc.vector.tensor_reduce(cum[:, 0, :], cmp[:], AXX, ALU.add))
                for k, d in enumerate((1, 2, 4)):
                    nc.vector.tensor_copy(cum[:, k + 1, 0:d], cum[:, k, 0:d])
                    link(nc.vector.tensor_tensor(cum[:, k + 1, d:E], cum[:, k, d:E], cum[:, k, 0:E - d], ALU.add))
                link(nc.vector.tensor_tensor(ucmp, spread_e(cum[:, 3, :]), spread_u(unit_no[:]), ALU.is_le))
                nc.vector.tensor_reduce(ue[:], ucmp, AXX, ALU.add)
                link(nc.vector.tensor_tensor(ucmp2, ucmp, spread_e(cum[:, 0, :]), ALU.mult))
                link(nc.vector.tensor_reduce(uw[:, 0, :], ucmp2, AXX, ALU.add))
                nc.vector.tensor_scalar(unit_expert[:], ue[:], float(E - 1), None, ALU.min).then_inc(table_ready, 1)
                link(nc.vector.tensor_tensor(uw[:, 1, :], unit_no[:], uw[:, 0, :], ALU.subtract))
                nc.vector.scalar_tensor_tensor(out=unit_block[:], in0=ue[:], scalar=float(BE), in1=uw[:, 1, :],
                                               op0=ALU.mult, op1=ALU.add).then_inc(table_ready, 1)

            nc.vector.memset(ones[:], 1.0)
            dve.wait_ge(consts, 3)
            nc.vector.tensor_copy(tri[:], tri32)
            nc.vector.tensor_copy(base[:], start0[:]).then_inc(consts, 1)
            dve.wait_ge(w_hi, 1)
            low(g_stage[:], Wg[0][:], Wg[1][:])
            dve.wait_ge(tanh_done, 1)
            nc.vector.tensor_scalar(gate[:, 2:3], gate[:, 1:2], 1.0 / (XS * WS), None, ALU.mult).then_inc(gate_ready, 1)
            dve.wait_ge(gate_ready, 1)
            dve.wait_ge(consts, 4)
            ROUTE_LINKS = 10

            def group(f, r, half):
                late = not known(f) or f > 0
                if late:
                    links.set((f - 1) * ROUTE_LINKS, 0)
                if late:
                    best_two(f - 1)
                for c in range(KC):
                    transposed_lo(f * KC, r, c, route_bank)
                if late:
                    places(f - 1, 1 - r, half - (1 - r))
                if r == 1:
                    since(dve, scattered[1], half * (TK * 16))

            groups(dve, group)
            links.set((B - 1) * ROUTE_LINKS, 0)
            best_two(B - 1)
            places(B - 1, 1, B // 2 - 1)
            assert links.value == B * ROUTE_LINKS, links.value
            unit_table()
            for j, n in enumerate("uvo"):
                for k in range(PARTS):
                    dve.wait_ge(w_hi, 1 + j * PARTS + (k + 1))
                    low(part(stage[n], k), part(W[n][0], k), part(W[n][1], k))
            for c in range(FU):
                transposed_lo(B * KC, 0, c, unit_bank)

            def unit(s, r, half):
                more = not known(s) or s < UNITS - 1
                dve.wait_ge(tanh_ready, s + 1)
                nc.vector.scalar_tensor_tensor(out=th[:, 0:UR], in0=th[:, 0:UR], scalar=1.0, in1=U[:, 0:UR],
                                               op0=ALU.add, op1=ALU.mult).then_inc(a_done, 1)
                if more:
                    for c in range(FU):
                        transposed_lo(s * FU + (B * KC + FU), 1 - r, c, unit_bank)
                dve.wait_ge(a_done, s + 1)
                dve.wait_ge(v_filled, s + 1)
                nc.vector.scalar_tensor_tensor(out=s32[:, 0:UR], in0=th[:, 0:UR], scalar=XS * 0.5 / (XS * WS) ** 2,
                                               in1=Vp[:, 0:UR], op0=ALU.mult, op1=ALU.mult).then_inc(s_done, 1)
                dve.wait_ge(s_hi, s + 1)
                half_of = slice(r * UR, (r + 1) * UR)
                nc.vector.tensor_tensor(sT[1][:, half_of], s32[:, 0:UR], sT[0][:, half_of], ALU.subtract).then_inc(s_lo, 1)

            units(dve, unit)

            link(nc.vector.tensor_scalar(y_step[:], cum[:, 0, 0:E - 1], float(UR), float(-ROWS), ALU.mult, ALU.add))
            link(nc.vector.tensor_tensor(y_cmp, pos_all[:].unsqueeze(2).to_broadcast([P, B * TK, E - 1]),
                                         start0[:, 1:E].unsqueeze(1).to_broadcast([P, B * TK, E - 1]), ALU.is_ge))
            link(nc.vector.tensor_tensor(y_cmp, y_cmp, y_step[:].unsqueeze(1).to_broadcast([P, B * TK, E - 1]),
                                         ALU.mult))
            link(nc.vector.tensor_reduce(y_off[:], y_cmp, AXX, ALU.add))
            nc.vector.tensor_tensor(y_pos[:], pos_all[:], y_off[:], ALU.add).then_inc(y_pos_ready, 1)

            def combine(g, q, use):
                dve.wait_ge(yg_ld[q], use * (2 * K * 16) + 2 * K * 16)
                since(dve, st[q], use * 16)
                w, x2 = cols(w_all, g, 2 * K), cols(x2_rows, g, 2)
                for t in range(2):
                    last = nc.vector.scalar_tensor_tensor(out=res(q)[:, t, :], in0=yg(q)[:, t * K, :],
                                                          scalar=w[:, t * K:t * K + 1], in1=x2[:, t, :],
                                                          op0=ALU.mult, op1=ALU.add)
                last.then_inc(half_done, 1)
                dve.wait_ge(half_done, g + 1)
                for t in range(2):
                    last = nc.vector.scalar_tensor_tensor(out=res(q)[:, t, :], in0=yg(q)[:, t * K + 1, :],
                                                          scalar=w[:, t * K + 1:t * K + 2], in1=res(q)[:, t, :],
                                                          op0=ALU.mult, op1=ALU.add)
                last.then_inc(out_ready, 1)

            pairs(dve, combine)

        @block.tensor
        def _(pe):
            PASSES = ((0, 0), (0, 1), (1, 0))

            def transposes(q, src, c):
                since(pe, m_free, q + (c + 1 - KC))
                for t in range(TT):
                    last = nc.tensor.transpose(route_bank(c)[:, t * P:(t + 1) * P], src[:, t, c * P:(c + 1) * P], ident[:])
                last.then_inc(m_filled, 1)

            def logits(f, r):
                pe.wait_ge(m_free, f * KC + KC)
                since(pe, l_free, f)
                parts = [(a, m, c) for c in range(KC) for a, m in PASSES + ((1, 1),)]
                for t in range(TT):
                    for k, (a, m, c) in enumerate(parts):
                        last = nc.tensor.matmul(L[:, t * E:(t + 1) * E], xT[a][:, r, c, t * P:(t + 1) * P],
                                                Wg[m][:, c, :], start=k == 0, stop=k == len(parts) - 1)
                last.then_inc(l_filled, 1)

            def ranks(f):
                pe.wait_ge(both_ready, f + 1)
                since(pe, pos_ready, f)
                for t in range(TT + 1):
                    for k in range(min(t + 1, TT)):
                        last = nc.tensor.matmul(RK[:, t * E:(t + 1) * E], tri[:] if k == t else ones[:], both[:, k, :],
                                                start=k == 0, stop=k == min(t, TT - 1))
                last.then_inc(rk_filled, 1)

            def group(f, r, half):
                pe.wait_ge(xn_ready, f + 1)
                for c in range(KC):
                    transposes(f * KC, xn[:, r], c)
                if not known(f) or f > 0:
                    ranks(f - 1)
                if known(f) and f == 0:
                    pe.wait_ge(w_ready, 1)
                    pe.wait_ge(consts, 4)
                logits(f, r)

            groups(pe, group)
            ranks(B - 1)

            def unit_transposes(q, src, c):
                since(pe, m_free, q + (c - 1))
                for j in range(TT):
                    chunk, t = (c * TT + j) // TU, j % TU
                    last = nc.tensor.transpose(unit_bank(c)[:, j * P:(j + 1) * P], src[:, t, chunk * P:(chunk + 1) * P],
                                               ident[:])
                last.then_inc(m_filled, 1)

            def up(n, dst, e, r, done):
                x_rows = [xT[a][:, r].rearrange("p c s -> p (c s)") for a in range(2)]
                parts = [(m, a, c) for c in range(KC) for m, a in PASSES]
                for k, (m, a, c) in enumerate(parts):
                    w = W[n][m][:, bass.ds(e, 1), c * P:(c + 1) * P].rearrange("p o n -> p (o n)")
                    last = nc.tensor.matmul(dst[:, 0:UR], w, x_rows[a][:, c * UR:(c + 1) * UR], start=k == 0, stop=k == len(parts) - 1)
                last.then_inc(done, 1)

            def expert_of(s):
                return pe.value_load(unit_expert[0:1, s:s + 1] if known(s) else unit_expert[0:1, bass.ds(s, 1)],
                                     min_val=0, max_val=E - 1)

            def down(s, r, e):
                pe.wait_ge(s_lo, s + 1)
                for t in range(TU):
                    since(pe, y_taken, s * TU + (t + 1 - TU))
                    for a, m in PASSES:
                        w = W["o"][m][:, bass.ds(e, 1), :].rearrange("p o n -> p (o n)")
                        last = nc.tensor.matmul(Y[:, r * TU + t, :], sT[a][:, (r * TU + t) * P:(r * TU + t + 1) * P], w,
                                                start=(a, m) == PASSES[0], stop=(a, m) == PASSES[-1])
                    last.then_inc(y_filled, 1)

            pe.wait_ge(table_ready, 1)
            pe.wait_ge(xg_ld[0], TU * 16)
            for c in range(FU):
                unit_transposes(B * KC, xg[:, 0], c)

            def unit(s, r, half):
                more = not known(s) or s < UNITS - 1
                e = expert_of(s)
                pe.wait_ge(m_free, s * FU + (B * KC + FU))
                since(pe, a_done, s)
                if known(s) and s == 0:
                    pe.wait_ge(w_ready, 1 + 3 * PARTS)
                up("u", U, e, r, u_filled)
                if more:
                    pe.wait_ge(xg_ld[1 - r], (half + r) * (TU * 16) + TU * 16)
                    for c in range(FU):
                        unit_transposes(s * FU + (B * KC + FU), xg[:, 1 - r], c)
                since(pe, s_done, s)
                up("v", Vp, e, r, v_filled)
                if not known(s) or s > 0:
                    down(s - 1, 1 - r, expert_of(s - 1))

            units(pe, unit)
            down(UNITS - 1, (UNITS - 1) % 2, expert_of(UNITS - 1))


def program(nc, x, ctx_1024, g_xattn, g_ffn, wq, wk, wv, wo, bo, gate_w, wu, wvf, wof, out):
    x2_dram = nc.dram_tensor("x2_scratch", tuple(x.shape), F32, kind="Internal").ap()
    with nc.sbuf_tensor("identity", [P, P], F32) as ident, nc.semaphore("identity_ready") as ident_ready, \
            nc.sbuf_tensor("x2_statistics", [P, x.shape[0] * x.shape[1] // P, 6], F32) as x2_stats, \
            nc.sbuf_tensor("ln_constants", [P, len(LN_CONSTANTS), x.shape[0] * x.shape[1] // P], F32) as ln_cst:
        with nc.Block() as block:
            @block.vector
            def _(dve):
                for k, value in enumerate(LN_CONSTANTS):
                    nc.vector.memset(ln_cst[:, k, :], value)

            @block.gpsimd
            def _(pool):
                nc.gpsimd.memset(ident[:], 1.0).then_inc(ident_ready, 1)
                pool.wait_ge(ident_ready, 1)
                nc.gpsimd.affine_select(out=ident[:], in_=ident[:], compare_op=ALU.is_equal, fill=0.0, base=0,
                                        pattern=[[-1, P]], channel_multiplier=1).then_inc(ident_ready, 1)
                pool.wait_ge(ident_ready, 2)
        attention_phase(nc, x, ctx_1024, g_xattn, wq, wk, wv, wo, bo, x2_dram, x2_stats, ident, ln_cst)
        ffn_phase(nc, x2_dram, x2_stats, g_ffn, gate_w, wu, wvf, wof, out, ident, ln_cst)


_INS = ["x", "ctx_1024", "g_xattn", "g_ffn", "L0_xattn_Wq", "L0_xattn_Wk", "L0_xattn_Wv", "L0_xattn_Wo",
        "L0_xattn_bo", "L0_ffn_gate_w", "L0_ffn_Wu", "L0_ffn_Wv", "L0_ffn_Wo"]


def kernel(**inputs):
    import numpy as _np
    import concourse.bacc as _bacc
    from concourse import mybir as _mybir
    from concourse.bass_utils import run_bass_kernel_spmd as _run

    nc = _bacc.Bacc("TRN2", target_bir_lowering=False, num_devices=1)
    arrays, args = {}, []
    for name in _INS:
        a = _np.ascontiguousarray(inputs[name])
        arrays[f"in_{name}_dram"] = a
        args.append(nc.dram_tensor(f"in_{name}_dram", a.shape, _mybir.dt.from_np(a.dtype), kind="ExternalInput").ap())
    out = nc.dram_tensor("out_0_dram", (8, 512, 512), _mybir.dt.float32, kind="ExternalOutput").ap()
    program(nc, *args, out)
    r = _run(nc, [arrays], core_ids=[0])
    return r.results[0]["out_0_dram"]
```
